# Optimizing a Trainium2 kernel written in Bass

```python
import numpy as np
import jax
import jax.numpy as jnp

def _softmax(x, axis=-1):
    return jax.nn.softmax(x, axis=axis)

def _gelu(x):
    return jax.nn.gelu(x, approximate=True)

def _silu(x):
    return jax.nn.silu(x)

def _sigmoid(x):
    return jax.nn.sigmoid(x)

def _layernorm(x, axis=-1, eps=1e-05):
    m = jnp.mean(x, axis=axis, keepdims=True)
    v = jnp.var(x, axis=axis, keepdims=True)
    return (x - m) / jnp.sqrt(v + eps)

def _scatter_add(tgt, idx, src, axis=0):
    return tgt.at[idx].add(src)

def _segment_sum(src, seg, n):
    return jax.ops.segment_sum(src, seg, n)
kernel_name = 'mk_adj_resnorm_d2_adj_r2_54c998'

def setup_inputs(seed: int=0):
    np.random.seed(seed)
    _w = jnp.asarray

    def _rec_inputs():
        import jax
        import jax.numpy as jnp
        _gk = jax.random.key(seed)
        x = -0.0002928 + 1 * jax.random.normal(jax.random.fold_in(_gk, 1), (8, 2048, 128), jnp.float32)
        _a = jax.random.bernoulli(jax.random.fold_in(_gk, 2), 0.0078125, (8, 2048, 2048))
        _a = jnp.logical_or(_a, jnp.swapaxes(_a, -1, -2))
        _a = jnp.logical_or(_a, jnp.eye(2048, dtype=bool))
        _af = _a.astype(jnp.float32)
        _af = _af * jax.random.uniform(jax.random.fold_in(_gk, 3), (8, 2048, 2048), jnp.float32, 0.05, 1)
        adj = _af
        return (x, adj)
    x, adj = _rec_inputs()

    def _L0_gnn_setup():
        import jax, jax.numpy as jnp
        import numpy as np
        ALPHA = 0.2
        MLP_ALPHA = 0.01
        EPS = 1e-05

        def leaky(x, a):
            return jnp.where(x >= 0, x, a * x)
        key = jax.random.key(seed)
        ks = jax.random.split(key, 12)
        B, N, FIN, FOUT, K = (4, 2048, 128, 128, 64)
        s = 0.05
        return {'h': jax.random.normal(ks[0], (B, N, FIN), jnp.float32), 'adj': jax.random.uniform(ks[1], (B, N, N), jnp.float32), 'W': jax.random.normal(ks[2], (FIN, FOUT), jnp.float32) * s, 'a': jax.random.normal(ks[3], (FOUT, 1), jnp.float32) * s, 'ln_g': jnp.ones((FOUT,), jnp.float32), 'ln_b': jnp.zeros((FOUT,), jnp.float32), 'W1': jax.random.normal(ks[4], (FOUT, FOUT), jnp.float32) * s, 'b1': jnp.zeros((FOUT,), jnp.float32), 'W2': jax.random.normal(ks[5], (FOUT, FOUT), jnp.float32) * s, 'b2': jnp.zeros((FOUT,), jnp.float32), 'W3': jax.random.normal(ks[6], (FOUT, FOUT), jnp.float32) * s, 'b3': jnp.zeros((FOUT,), jnp.float32), 'k': K}
    _L0_gnn_all = _L0_gnn_setup()
    _L0_gnn_in = {k: v for k, v in _L0_gnn_all.items() if k in ('W', 'a', 'ln_g', 'ln_b', 'W1', 'b1', 'W2', 'b2', 'W3', 'b3')}
    del _L0_gnn_all

    def _L1_gnn_setup():
        import jax, jax.numpy as jnp
        import numpy as np
        H = 4
        NEG = -9000000000000000.0
        key = jax.random.key(seed)
        k1, k2, k3, k4 = jax.random.split(key, 4)
        B, N, D = (8, 512, 128)
        dh = D // H
        return {'node_features': jax.random.normal(k1, (B, N, D), dtype=jnp.float32), 'adjacency': jax.random.uniform(k2, (B, N, N), dtype=jnp.float32), 'W_proj': jax.random.normal(k3, (D, D), dtype=jnp.float32) * (1.0 / np.sqrt(D)), 'a_w': jax.random.normal(k4, (1, 2 * dh + 1), dtype=jnp.float32) * 0.1, 'bias': jnp.zeros((D,), dtype=jnp.float32)}
    _L1_gnn_all = _L1_gnn_setup()
    _L1_gnn_in = {k: v for k, v in _L1_gnn_all.items() if k in ('W_proj', 'a_w', 'bias')}
    del _L1_gnn_all
    return {'x': x, 'adj': adj, 'L0_gnn_W': _L0_gnn_in['W'], 'L0_gnn_a': _L0_gnn_in['a'], 'L0_gnn_ln_g': _L0_gnn_in['ln_g'], 'L0_gnn_ln_b': _L0_gnn_in['ln_b'], 'L0_gnn_W1': _L0_gnn_in['W1'], 'L0_gnn_b1': _L0_gnn_in['b1'], 'L0_gnn_W2': _L0_gnn_in['W2'], 'L0_gnn_b2': _L0_gnn_in['b2'], 'L0_gnn_W3': _L0_gnn_in['W3'], 'L0_gnn_b3': _L0_gnn_in['b3'], 'L1_gnn_W_proj': _L1_gnn_in['W_proj'], 'L1_gnn_a_w': _L1_gnn_in['a_w'], 'L1_gnn_bias': _L1_gnn_in['bias']}

def reference(x, adj, L0_gnn_W, L0_gnn_a, L0_gnn_ln_g, L0_gnn_ln_b, L0_gnn_W1, L0_gnn_b1, L0_gnn_W2, L0_gnn_b2, L0_gnn_W3, L0_gnn_b3, L1_gnn_W_proj, L1_gnn_a_w, L1_gnn_bias):
    import jax
    import jax.numpy as jnp

    def _L0_gnn_ref(h, adj, W, a, ln_g, ln_b, W1, b1, W2, b2, W3, b3, k):
        import jax, jax.numpy as jnp
        import numpy as np
        ALPHA = 0.2
        MLP_ALPHA = 0.01
        EPS = 1e-05

        def leaky(x, a):
            return jnp.where(x >= 0, x, a * x)
        Wh = h @ W
        B, N, Fd = Wh.shape
        C = N // k
        Whc = Wh.reshape(B, C, k, Fd)
        e = leaky(jnp.squeeze(Whc @ a, -1), ALPHA)
        idx = jnp.arange(C)
        blocks = adj.reshape(B, C, k, C, k)[:, idx, :, idx, :]
        blocks = jnp.transpose(blocks, (1, 0, 2, 3))
        scores = jax.nn.softmax(blocks * e[..., :, None], axis=-1)
        out = jnp.einsum('bcij,bcjf->bcif', scores, Whc)
        y = leaky(out @ W1 + b1, MLP_ALPHA)
        y = leaky(y @ W2 + b2, MLP_ALPHA)
        y = y @ W3 + b3
        z = y + out
        mu = jnp.mean(z, axis=-1, keepdims=True)
        var = jnp.var(z, axis=-1, keepdims=True)
        z = (z - mu) / jnp.sqrt(var + EPS) * ln_g + ln_b
        return z.reshape(B, N, Fd)

    def _L1_gnn_ref(node_features, adjacency, W_proj, a_w, bias):
        import jax, jax.numpy as jnp
        import numpy as np
        H = 4
        NEG = -9000000000000000.0
        B, N, D = node_features.shape
        dh = D // H
        h = (node_features @ W_proj.T).reshape(B, N, H, dh)
        w = a_w[0]
        wl, wr, we = (w[:dh], w[dh:2 * dh], w[2 * dh])
        s_left = jnp.einsum('bihd,d->bih', h, wl)
        s_right = jnp.einsum('bjhd,d->bjh', h, wr)
        scores = s_left[:, :, None, :] + s_right[:, None, :, :] + adjacency[..., None] * we
        scores = jax.nn.leaky_relu(scores, negative_slope=0.2)
        pad = (adjacency <= 1e-05).astype(scores.dtype)
        scores = scores + (NEG * pad)[..., None]
        attn = jax.nn.softmax(scores, axis=2)
        agg = jnp.einsum('bijh,bjhd->bihd', attn, h).reshape(B, N, D)
        out = jax.nn.leaky_relu(node_features + agg + bias, negative_slope=0.5)
        return out
    x = _layernorm(x + _L0_gnn_ref(x, adj, L0_gnn_W, L0_gnn_a, L0_gnn_ln_g, L0_gnn_ln_b, L0_gnn_W1, L0_gnn_b1, L0_gnn_W2, L0_gnn_b2, L0_gnn_W3, L0_gnn_b3, 64), axis=-1)
    x = _layernorm(x + _L1_gnn_ref(x, adj, L1_gnn_W_proj, L1_gnn_a_w, L1_gnn_bias), axis=-1)
    return x

_drawn_inputs = setup_inputs


def setup_inputs(seed=0):
    import zlib

    import numpy as np

    out = dict(_drawn_inputs(seed))
    spreads = {'L0_gnn_ln_g': (1.0, 0.2),
     'L0_gnn_ln_b': (0.0, 0.1),
     'L0_gnn_b1': (0.0, 0.1),
     'L0_gnn_b2': (0.0, 0.1),
     'L0_gnn_b3': (0.0, 0.1),
     'L1_gnn_bias': (0.0, 0.1)}
    factors = {'L0_gnn_a': 5.338}
    for name, (base, spread) in spreads.items():
        noise = np.random.default_rng([zlib.crc32(name.encode()), seed]).standard_normal(out[name].shape)
        drawn = base * np.exp(spread * noise) if base else spread * noise
        out[name] = jnp.asarray(drawn.astype(out[name].dtype))
    for name, factor in factors.items():
        out[name] = (out[name] * factor).astype(out[name].dtype)
    return out
```

```python
import concourse.bass as bass
from concourse import mybir
from contextlib import ExitStack


def build_program(nc, x, adj, W, a, ln_g, ln_b, W1, b1, W2, b2, W3, b3, W_proj, a_w, bias, out):
    fp32 = mybir.dt.float32
    bf16 = mybir.dt.bfloat16
    ALU = mybir.AluOpType
    ACT = mybir.ActivationFunctionType
    AX_X = mybir.AxisListType.X

    B, N, D = x.shape
    P = 128
    DH = (a_w.shape[1] - 1) // 2
    H = D // DH
    K = 64
    GT = 4
    GROUP = GT * P
    NB = N // GROUP
    NG = B * NB
    JT = N // P
    HA = DH + 1
    HR = D + H
    CHUNK = 4
    NC_ = JT // CHUNK
    EPS = 1e-5
    PAD = 1.0000001111620804e-05
    BIG = 2.0 ** 100
    TINY = 1e-30
    LAG = 2

    x1_d = nc.dram_tensor("x1_scratch", [NG, P, GT * D], fp32).ap()
    h_d = nc.dram_tensor("h_scratch", [NG, P, GT * HR], fp32).ap()
    sl_d = nc.dram_tensor("left_scratch", [NG, H, GROUP], fp32).ap()

    x_g = x.rearrange("b (g t p) f -> (b g) p t f", p=P, t=GT)
    out_g = out.rearrange("b (g t p) f -> (b g) p t f", p=P, t=GT)
    h_b = h_d.rearrange("(b g) p c -> b p g c", g=NB)
    sl_b = sl_d.rearrange("(b g) h i -> b h g i", g=NB)
    adj_g = adj.rearrange("b (g t p) j -> (b g) p t j", p=P, t=GT)

    ctx = ExitStack()
    with ctx:
        def sb(name, shape, dt=fp32):
            return ctx.enter_context(nc.sbuf_tensor(name, shape, dt))

        def sem(name):
            return ctx.enter_context(nc.semaphore(name))

        def bc(ap, axis, shape):
            return ap.unsqueeze(axis).broadcast_to(shape)

        ident = sb("ident", [P, P])
        ones = sb("ones", [H, P])
        ones_row = sb("ones_row", [1, GROUP])
        tiny = sb("tiny", [P, 1])
        mhalf = sb("mhalf", [P, GT])
        eps_c = sb("eps_c", [P, GT])
        pen_bias = sb("pen_bias", [P, 1])
        sgn_ident = sb("sgn_ident", [P, P], bf16)
        we_raw = sb("we_raw", [P, 1])
        we_s = sb("we_s", [P, 8])
        sel = sb("sel", [P, H, P])
        W_sb = sb("W_sb", [P, D + 1])
        WT = sb("WT", [P, D])
        a_sb = sb("a_sb", [P, 1])
        W1_sb = sb("W1_sb", [P, D])
        W2_sb = sb("W2_sb", [P, D])
        W3_sb = sb("W3_sb", [P, D])
        b1_sb = sb("b1_sb", [P, 1])
        b2_sb = sb("b2_sb", [P, 1])
        b3_row = sb("b3_row", [1, D])
        g_bc = sb("g_bc", [P, D])
        b_bc = sb("b_bc", [P, D])
        bias_bc = sb("bias_bc", [P, D])
        Wp_sb = sb("Wp_sb", [P, D])
        WpT = sb("WpT", [P, HR])
        Wsl = sb("Wsl", [P, H])
        wlr = sb("wlr", [P, 2 * H])

        U2 = range(2)
        xg = [sb(f"xg{u}", [P, GT, D]) for u in U2]
        blk = [sb(f"blk{u}", [P, GT, K]) for u in U2]
        xT = [sb(f"xT{u}", [P, GROUP]) for u in U2]
        whe = [sb(f"whe{u}", [P, GT, D + 1]) for u in U2]
        e_l = [sb(f"e_l{u}", [P, GT]) for u in U2]
        ex = [sb(f"ex{u}", [P, GT, K]) for u in U2]
        rmx = [sb(f"rmx{u}", [P, GT]) for u in U2]
        rsm = [sb(f"rsm{u}", [P, GT]) for u in U2]
        S = [sb(f"S{u}", [P, GT, P]) for u in U2]
        ST = [sb(f"ST{u}", [P, GROUP]) for u in U2]
        oT = [sb(f"oT{u}", [P, GROUP]) for u in U2]
        yb = [sb(f"yb{u}", [P, GROUP]) for u in U2]
        y1T = [sb(f"y1T{u}", [P, GROUP]) for u in U2]
        y2T = [sb(f"y2T{u}", [P, GROUP]) for u in U2]
        zn = [sb(f"zn{u}", [P, GT, D]) for u in U2]
        st6 = [sb(f"st6{u}", [P, GT, 6]) for u in U2]
        mv = [sb(f"mv{u}", [P, GT, 2]) for u in U2]
        ve = [sb(f"ve{u}", [P, GT]) for u in U2]
        rstd = [sb(f"rstd{u}", [P, GT]) for u in U2]
        x1 = [sb(f"x1{u}", [P, GT, D]) for u in U2]
        x1T = [sb(f"x1T{u}", [P, GROUP]) for u in U2]
        h_o = [sb(f"h_o{u}", [P, GT, HR]) for u in U2]
        sl_o = [sb(f"sl_o{u}", [H, GROUP]) for u in U2]

        NF = 4
        NX = 4
        NPEN = 4
        adj_sb = [sb(f"adj_sb{c}", [P, GT, CHUNK * P]) for c in range(NC_)]
        pen = [sb(f"pen{r}", [P, GT, P], bf16) for r in range(NPEN)]
        F = [sb(f"F{r}", [P, GROUP]) for r in range(NF)]
        E = [sb(f"E{r}", [P, GROUP]) for r in range(NF)]
        X = [sb(f"X{r}", [P, H, GROUP]) for r in range(NX)]
        hb = sb("hb", [P, JT, HR])
        left = sb("left", [H, N])
        rho4 = sb("rho4", [P, N])
        rm = sb("rm", [P, H])
        R4 = sb("R4", [H, 1])
        R4W = sb("R4W", [H, 1])
        diagR = sb("diagR", [H, H])
        Rb = sb("Rb", [P, H])
        sig = sb("sig", [P, JT, H])
        s_j = sb("s_j", [P, JT, H])
        v_j = sb("v_j", [P, JT, H])
        haug = sb("haug", [P, JT, H, HA])
        hmean = sb("hmean", [1, H, HA])
        accU = sb("accU", [P, 2, GROUP])
        natO = sb("natO", [P, 2, GT, P])
        rden = sb("rden", [P, 2, GT, 2])
        x1b = sb("x1b", [P, GT, D])
        res = sb("res", [P, GT, D])
        lky = sb("lky", [P, GT, D])
        est6 = sb("est6", [P, GT, 6])
        emv = sb("emv", [P, GT, 2])
        eve = sb("eve", [P, GT])
        erstd = sb("erstd", [P, GT])
        o_sb = sb("o_sb", [P, GT, D])

        psum = ctx.enter_context(nc.psum_tensor("psum", [P, 8, GROUP], fp32))
        bank = [psum[:, i, :] for i in range(8)]
        BANKS = [bank[0:4], bank[4:8]]
        RHO = bank[0:4]
        TA = bank[4:6]
        ACC = bank[6:8]

        const_set = sem("const_set")
        weights_in = sem("weights_in")
        prep_pe = sem("prep_pe")
        prep_dve = sem("prep_dve")
        prep_act = sem("prep_act")
        x_in = [sem(f"x_in{u}") for u in U2]
        xT_ps = sem("xT_ps")
        xT_sb = sem("xT_sb")
        wh_ps = sem("wh_ps")
        scores_sb = sem("scores_sb")
        exp_sb = sem("exp_sb")
        soft_sb = sem("soft_sb")
        ST_ps = sem("ST_ps")
        ST_sb = sem("ST_sb")
        oT_ps = sem("oT_ps")
        oT_sb = sem("oT_sb")
        y1_ps = sem("y1_ps")
        y1_b = sem("y1_b")
        y1_sb = sem("y1_sb")
        y2_ps = sem("y2_ps")
        y2_b = sem("y2_b")
        y2_sb = sem("y2_sb")
        z_ps = sem("z_ps")
        var_z = sem("var_z")
        rstd_z = sem("rstd_z")
        zn_sb = sem("zn_sb")
        r_sb = [sem(f"r_sb{u}") for u in U2]
        var_r = sem("var_r")
        rstd_r = sem("rstd_r")
        x1_sb = [sem(f"x1_sb{u}") for u in U2]
        x1T_ps = sem("x1T_ps")
        x1T_sb = sem("x1T_sb")
        h_ps = sem("h_ps")
        h_sb = [sem(f"h_sb{u}") for u in U2]
        stored = [sem(f"stored{u}") for u in U2]
        dve0 = sem("dve0")
        pool0 = sem("pool0")
        adj_in = [sem(f"adj_in{c}") for c in range(NC_)]
        pen_sb = sem("pen_sb")
        adjT_ps = sem("adjT_ps")
        F_sb = sem("F_sb")
        E_sb = sem("E_sb")
        X_sb = sem("X_sb")
        P_pool = sem("P_pool")
        P_dve = sem("P_dve")
        pv_done = sem("pv_done")
        rho_ps = sem("rho_ps")
        accU_sb = sem("accU_sb")
        nat_ps = sem("nat_ps")
        nat_sb = sem("nat_sb")
        hb_in = sem("hb_in")
        rm_sb = sem("rm_sb")
        rmT_ps = sem("rmT_ps")
        diag_sb = sem("diag_sb")
        Rb_ps = sem("Rb_ps")
        sig_sb = sem("sig_sb")
        sv_sb = sem("sv_sb")
        left_sb = sem("left_sb")
        rho_sb = sem("rho_sb")
        haug_sb = sem("haug_sb")
        hsum_ps = sem("hsum_ps")
        hmean_sb = sem("hmean_sb")
        res_sb = sem("res_sb")
        x1_in = sem("x1_in")
        evar = sem("evar")
        erstd_sb = sem("erstd_sb")
        o_done = sem("o_done")
        out_st = sem("out_st")
        dve_b = sem("dve_b")
        dve_e = sem("dve_e")
        pool_e = sem("pool_e")

        N_WEIGHTS = 13 + 2 * H
        N_CONST = 15
        POOL0, DVE0, DVE_B, DVE_E = 8, 14, 3, 5

        def chain(eng, semaphore, base):
            count = [0]

            def link(ins):
                count[0] += 1
                ins.then_inc(semaphore, 1)
                eng.wait_ge(semaphore, base + count[0])
            return link, count

        HEAD = 8

        def walk(eng, batch, tile, epilogue):
            def step(b, g, ib, crossing):
                for k in range(HEAD, JT):
                    tile(b, g, ib, k, crossing)
                if crossing:
                    batch(b + 1)
                for k in range(HEAD):
                    tile(b + 1 if crossing else b, g + 1, 0 if crossing else ib + 1, k, False)
                    epilogue(g, k)

            batch(0)
            for k in range(HEAD):
                tile(0, 0, 0, k, False)
            with eng.Fori(0, B - 1) as b:
                with eng.Fori(0, NB - 1) as ib:
                    step(b, b * NB + ib, ib, False)
                step(b, b * NB + (NB - 1), NB - 1, True)
            with eng.Fori(0, NB - 1) as ib:
                step(B - 1, ib + (B - 1) * NB, ib, False)
            for k in range(HEAD, JT):
                tile(B - 1, NG - 1, NB - 1, k, False)
            for k in range(HEAD):
                epilogue(NG - 1, k)

        def is_last(g):
            return isinstance(g, int) and g == NG - 1

        block = ctx.enter_context(nc.Block())

        @block.sync
        def _(sp):
            for dst, src in ((W_sb[:, 0:D], W), (a_sb[:], a), (W1_sb[:], W1), (W2_sb[:], W2), (W3_sb[:], W3),
                             (b1_sb[:], b1.unsqueeze(1)), (b2_sb[:], b2.unsqueeze(1)), (b3_row[:], b3.unsqueeze(0)),
                             (g_bc[:], ln_g.partition_broadcast(P)), (b_bc[:], ln_b.partition_broadcast(P)),
                             (bias_bc[:], bias.partition_broadcast(P)), (Wp_sb[:], W_proj),
                             (we_raw[:], a_w[0, 2 * DH:2 * DH + 1].partition_broadcast(P))):
                sp.dma_start(dst, src).then_inc(weights_in, 16)
            sp.wait_ge(const_set, 1)
            for h in range(H):
                for side in range(2):
                    sp.dma_start(wlr[h * DH:(h + 1) * DH, side * H + h:side * H + h + 1],
                                 a_w[0, side * DH:(side + 1) * DH].unsqueeze(1)).then_inc(weights_in, 16)

            sp.sem_inc(res_sb, 1)
            sp.sem_inc(out_st, 1)
            for u in U2:
                sp.sem_inc(r_sb[u], 1)
                sp.sem_inc(h_sb[u], 1)
                sp.sem_inc(stored[u], 1)

            with sp.Fori(0, B) as b:
                with sp.Fori(0, NB // 2) as pr:
                    it = b * (NB // 2) + pr
                    for u in U2:
                        sp.wait_ge(r_sb[u], it + 1)
                        sp.dma_start(xg[u][:], x_g[it * 2 + u]).then_inc(x_in[u], 16)
                        for q in range(2):
                            at = b * (N * N) + pr * (2 * GROUP * (N + 1)) + (u * GROUP + q * K) * (N + 1)
                            sp.dma_start(blk[u][q * K:(q + 1) * K],
                                         bass.AP(adj.tensor, at, [[N, K], [P * (N + 1), GT], [1, K]])) \
                                .then_inc(x_in[u], 16)

            def load_adj(g, c):
                sp.dma_start(adj_sb[c][:], adj_g[g][:, :, c * CHUNK * P:(c + 1) * CHUNK * P]).then_inc(adj_in[c], 16)

            LOAD_AT = (HEAD, HEAD + 1, HEAD + 4, HEAD + 6)

            def load_batch(b):
                sp.dma_start(hb[:].rearrange("p (g t) c -> p g (t c)", g=NB), h_b[b]).then_inc(hb_in, 16)
                sp.dma_start(left[:].rearrange("h (g i) -> h g i", g=NB), sl_b[b]).then_inc(hb_in, 16)

            for c in range(NC_):
                load_adj(0, c)
            for u in U2:
                sp.wait_ge(stored[u], 3 * 16 * (NG // 2) + 1)
            load_batch(0)
            sp.dma_start(x1b[:], x1_d[0]).then_inc(x1_in, 16)

            def batch(b):
                pass

            def tile(b, g, ib, k, crossing):
                if k in LOAD_AT and not is_last(g):
                    c = LOAD_AT.index(k)
                    sp.wait_ge(adjT_ps, JT * g + CHUNK * (c + 1))
                    load_adj(g + 1, c)
                if k == HEAD + 2 and crossing:
                    sp.wait_ge(haug_sb, 2 * (b + 1))
                    sp.wait_ge(hsum_ps, b + 1)
                    sp.wait_ge(rho_sb, b + 1)
                    load_batch(b + 1)

            def epilogue(g, k):
                if k == HEAD - 1:
                    sp.wait_ge(o_done, GT * (g + 1))
                    sp.dma_start(out_g[g], o_sb[:]).then_inc(out_st, 16)
                    if not is_last(g):
                        sp.dma_start(x1b[:], x1_d[g + 1]).then_inc(x1_in, 16)

            walk(sp, batch, tile, epilogue)
            sp.wait_ge(out_st, 16 * NG + 1)

        @block.gpsimd
        def _(pool):
            nc.gpsimd.memset(wlr[:], 0.0).then_inc(const_set, 1)
            nc.gpsimd.memset(ident[:], 0.0).then_inc(const_set, 1)
            nc.gpsimd.memset(sel[:], 1.0).then_inc(const_set, 1)
            nc.gpsimd.memset(ones[:], 1.0).then_inc(const_set, 1)
            nc.gpsimd.memset(ones_row[:], 1.0).then_inc(const_set, 1)
            nc.gpsimd.memset(tiny[:], TINY).then_inc(const_set, 1)
            nc.gpsimd.memset(mhalf[:], -0.5).then_inc(const_set, 1)
            nc.gpsimd.memset(eps_c[:], EPS).then_inc(const_set, 1)
            nc.gpsimd.memset(rho4[:], 0.0).then_inc(const_set, 1)
            nc.gpsimd.memset(hmean[:], N * TINY).then_inc(const_set, 1)
            nc.gpsimd.memset(accU[:], 0.0).then_inc(const_set, 1)
            for u in U2:
                nc.gpsimd.memset(S[u][:], 0.0).then_inc(const_set, 1)
            pool.wait_ge(const_set, 13)
            nc.gpsimd.affine_select(out=ident[:], in_=ident[:], compare_op=ALU.not_equal, fill=1.0, base=0,
                                    pattern=[[-1, P]], channel_multiplier=1).then_inc(const_set, 1)
            nc.gpsimd.affine_select(out=sel[:], in_=sel[:], compare_op=ALU.is_equal, fill=0.0, base=0,
                                    pattern=[[-1, H], [0, P]], channel_multiplier=1).then_inc(const_set, 1)

            pool.wait_ge(weights_in, 16 * N_WEIGHTS)
            with pool.Fori(0, NG // 2) as it:
                link, steps = chain(pool, pool0, it * POOL0)
                for u in U2:
                    pool.wait_ge(var_z, GT * (2 * it + u + 1))
                    link(nc.gpsimd.tensor_tensor(ve[u][:], mv[u][:, :, 1], eps_c[:], ALU.add))
                    nc.gpsimd.tensor_tensor(rstd[u][:], ve[u][:], mhalf[:], ALU.pow).then_inc(rstd_z, 1)
                for u in U2:
                    pool.wait_ge(zn_sb, GT * (2 * it + u + 1))
                    link(nc.gpsimd.tensor_tensor(zn[u][:], zn[u][:], bc(g_bc[:], 1, [P, GT, D]), ALU.mult))
                    link(nc.gpsimd.tensor_tensor(zn[u][:], zn[u][:], bc(b_bc[:], 1, [P, GT, D]), ALU.add))
                    nc.gpsimd.tensor_tensor(zn[u][:], zn[u][:], xg[u][:], ALU.add).then_inc(r_sb[u], 1)
                for u in U2:
                    pool.wait_ge(var_r, GT * (2 * it + u + 1))
                    link(nc.gpsimd.tensor_tensor(ve[u][:], mv[u][:, :, 1], eps_c[:], ALU.add))
                    nc.gpsimd.tensor_tensor(rstd[u][:], ve[u][:], mhalf[:], ALU.pow).then_inc(rstd_r, 1)
                assert steps[0] == POOL0

            def batch(b):
                pass

            def tile(b, g, ib, k, crossing):
                m = JT * g + k
                pool.wait_ge(X_sb, H * m + H - 1)
                pool.wait_ge(E_sb, m + 1)
                part = X[k % NX][:, 0:H - 1, :]
                nc.gpsimd.tensor_tensor(part, part, bc(E[k % NF][:], 1, [P, H - 1, GROUP]),
                                        ALU.mult).then_inc(P_pool, 1)

            def epilogue(g, k):
                if k == 6:
                    pool.wait_ge(evar, GT * (g + 1))
                    nc.gpsimd.tensor_tensor(eve[:], emv[:, :, 1], eps_c[:], ALU.add).then_inc(pool_e, 1)
                    pool.wait_ge(pool_e, g + 1)
                    nc.gpsimd.tensor_tensor(erstd[:], eve[:], mhalf[:], ALU.pow).then_inc(erstd_sb, 1)

            walk(pool, batch, tile, epilogue)

        @block.scalar
        def _(act):
            def copy(dst, src):
                return nc.scalar.activation(dst, src, ACT.Copy)

            act.wait_ge(prep_pe, 1)
            copy(WT[:], bank[0][:, 0:D]).then_inc(prep_act, 1)
            act.wait_ge(prep_pe, 2)
            copy(WpT[:, 0:D], bank[1][:, 0:D]).then_inc(prep_act, 1)
            act.wait_ge(prep_pe, 3)
            copy(Wsl[:], bank[2][:, 0:H]).then_inc(prep_act, 1)
            copy(WpT[:, D:HR], bank[2][:, H:2 * H]).then_inc(prep_act, 1)
            act.wait_ge(prep_pe, 4)
            copy(W_sb[:, D:D + 1], bank[3][:, 0:1]).then_inc(prep_act, 1)

            with act.Fori(0, NG // 2) as it:
                n = [2 * it + u + 1 for u in U2]
                for u in U2:
                    act.wait_ge(xT_ps, n[u])
                    copy(xT[u][:], BANKS[u][0]).then_inc(xT_sb, 1)
                for u in U2:
                    act.wait_ge(scores_sb, n[u])
                    nc.scalar.activation(ex[u][:], ex[u][:], ACT.Exp).then_inc(exp_sb, 1)
                for u in U2:
                    act.wait_ge(ST_ps, n[u])
                    copy(ST[u][:], BANKS[u][0]).then_inc(ST_sb, 1)
                for u in U2:
                    act.wait_ge(oT_ps, n[u])
                    copy(oT[u][:], BANKS[u][3]).then_inc(oT_sb, 1)
                for u in U2:
                    act.wait_ge(y1_ps, n[u])
                    nc.scalar.activation(yb[u][:], BANKS[u][0], ACT.Identity, bias=b1_sb[:]).then_inc(y1_b, 1)
                for u in U2:
                    act.wait_ge(y2_ps, n[u])
                    nc.scalar.activation(yb[u][:], BANKS[u][3], ACT.Identity, bias=b2_sb[:]).then_inc(y2_b, 1)
                for u in U2:
                    act.wait_ge(x1_sb[u], GT * (it + 1))
                    act.dma_start(x1_d[2 * it + u], x1[u][:].rearrange("p t f -> p (t f)")).then_inc(stored[u], 16)
                    act.wait_ge(x1T_ps, n[u])
                    copy(x1T[u][:], BANKS[u][2]).then_inc(x1T_sb, 1)
                for u in U2:
                    act.wait_ge(h_ps, n[u])
                    act.wait_ge(stored[u], 3 * 16 * it + 1)
                    for half, bk in ((0, 1), (1, 3)):
                        copy(h_o[u][:, 2 * half:2 * half + 2, :],
                             BANKS[u][bk][:, 0:2 * HR].rearrange("p (t c) -> p t c", t=2)).then_inc(h_sb[u], 1)
                    copy(sl_o[u][:], BANKS[u][0][0:H, :]).then_inc(h_sb[u], 1)
                for u in U2:
                    act.wait_ge(h_sb[u], 3 * it + 4)
                    act.dma_start(h_d[2 * it + u], h_o[u][:].rearrange("p t c -> p (t c)")).then_inc(stored[u], 16)
                    act.dma_start(sl_d[2 * it + u], sl_o[u][:]).then_inc(stored[u], 16)

            act.wait_ge(prep_dve, 11)

            def penalty(g, k):
                c = k // CHUNK
                act.wait_ge(adj_in[c], 16 * (g + 1))
                if not (isinstance(g, int) and g == 0 and k < NPEN):
                    act.wait_ge(adjT_ps, JT * g + k - NPEN + 1)
                nc.scalar.activation(pen[k % NPEN][:], adj_sb[c][:, :, (k % CHUNK) * P:(k % CHUNK + 1) * P],
                                     ACT.Relu, scale=-BIG, bias=pen_bias[:]).then_inc(pen_sb, 1)

            for k in range(NPEN):
                penalty(0, k)

            def batch(b):
                act.wait_ge(sig_sb, b + 1)
                act.wait_ge(X_sb, H * JT * NB * b)
                nc.scalar.activation(s_j[:], sig[:], ACT.Exp, scale=0.8).then_inc(sv_sb, 1)
                nc.scalar.activation(v_j[:], sig[:], ACT.Exp, scale=0.2).then_inc(sv_sb, 1)
                act.wait_ge(left_sb, b + 1)
                act.wait_ge(rho_ps, H * NB * b)
                nc.scalar.activation(rho4[0:H, :], left[:], ACT.Exp, scale=-0.8).then_inc(rho_sb, 1)
                act.wait_ge(hsum_ps, b + 1)
                act.wait_ge(pv_done, JT * NB * b)
                nc.scalar.activation(hmean[:, :, 0:DH], RHO[2][0:1, 0:D].rearrange("p (h d) -> p h d", h=H),
                                     ACT.Copy).then_inc(hmean_sb, 1)

            def tile(b, g, ib, k, crossing):
                m = JT * g + k
                early = isinstance(g, int) and g == 0 and k < NF
                act.wait_ge(adjT_ps, m + 1)
                if not early:
                    act.wait_ge(X_sb, H * (m - NF + 1))
                nc.scalar.activation(F[k % NF][:], TA[k % 2], ACT.Exp, scale=we_s[:, 3:4],
                                     bias=we_s[:, 4:5]).then_inc(F_sb, 1)
                if not early:
                    act.wait_ge(P_pool, m - NF + 1)
                    act.wait_ge(P_dve, m - NF + 1)
                nc.scalar.activation(E[k % NF][:], TA[k % 2], ACT.Exp, scale=we_s[:, 5:6],
                                     bias=we_s[:, 6:7]).then_inc(E_sb, 1)
                if k + NPEN < JT:
                    penalty(g, k + NPEN)
                elif not is_last(g):
                    penalty(g + 1, k + NPEN - JT)

            def epilogue(g, k):
                if k == 2:
                    act.wait_ge(pv_done, JT * (g + 1))
                    for a_ in range(2):
                        rows = slice(64 * a_, 64 * a_ + HA)
                        copy(accU[rows], psum[rows, 6:8, :]).then_inc(accU_sb, 1)
                if k == 3:
                    act.wait_ge(res_sb, 2 * g + 1)
                    for r in range(2):
                        act.wait_ge(nat_ps, 2 * g + r + 1)
                        copy(natO[:, r].rearrange("p t f -> p (t f)"), TA[r]).then_inc(nat_sb, 1)

            walk(act, batch, tile, epilogue)

        @block.vector
        def _(dve):
            V = nc.vector
            dve.wait_ge(weights_in, 16 * N_WEIGHTS)
            dve.wait_ge(const_set, N_CONST)
            link, _ = chain(dve, prep_dve, 0)
            w = [we_s[:, i:i + 1] for i in range(8)]
            link(V.tensor_scalar(w[0], we_raw[:], 0.0, 2.0, ALU.is_ge, ALU.mult))
            link(V.tensor_scalar(w[0], w[0], -1.0, None, ALU.add))
            link(V.tensor_scalar(w[1], we_raw[:], w[0], 1e-10, ALU.mult, ALU.max))
            link(V.tensor_scalar(w[2], w[1], w[0], None, ALU.mult))
            link(V.tensor_scalar(w[7], w[2], 0.0, None, ALU.max))
            link(V.tensor_scalar(w[3], w[2], 0.8, None, ALU.mult))
            link(V.tensor_scalar(w[5], w[2], 0.2, None, ALU.mult))
            link(V.tensor_scalar(w[4], w[7], -0.8, None, ALU.mult))
            link(V.tensor_scalar(w[6], w[7], -0.2, None, ALU.mult))
            link(V.tensor_scalar(sgn_ident[:], ident[:], w[0], -1.0, ALU.mult, ALU.mult))
            link(V.memset(pen_bias[:], BIG * PAD))

            def normalise(link, src, stats, mean_var, done):
                for t in range(GT):
                    V.bn_stats(stats[:, t, :], src(t))
                dve.drain()
                for t in range(GT):
                    V.bn_aggr(mean_var[:, t, :], stats[:, t, :]).then_inc(done, 1)

            with dve.Fori(0, NG // 2) as it:
                link, steps = chain(dve, dve0, it * DVE0)
                n = [2 * it + u + 1 for u in U2]
                for u in U2:
                    dve.wait_ge(wh_ps, n[u])
                    for half in range(2):
                        link(V.tensor_copy(whe[u][:, 2 * half:2 * half + 2, :],
                                           BANKS[u][1 + half][:, 0:2 * (D + 1)].rearrange("p (t c) -> p t c", t=2)))
                    link(V.scalar_tensor_tensor(e_l[u][:], whe[u][:, :, D], 0.2, whe[u][:, :, D], ALU.mult, ALU.max))
                    dve.wait_ge(x_in[u], 3 * 16 * (it + 1))
                    link(V.tensor_tensor(ex[u][:], blk[u][:], bc(e_l[u][:], 2, [P, GT, K]), ALU.mult))
                    link(V.reduce_max(rmx[u][:], ex[u][:], AX_X))
                    V.tensor_tensor(ex[u][:], ex[u][:], bc(rmx[u][:], 2, [P, GT, K]),
                                    ALU.subtract).then_inc(scores_sb, 1)
                for u in U2:
                    dve.wait_ge(exp_sb, n[u])
                    link(V.reduce_sum(rsm[u][:], ex[u][:], AX_X))
                    link(V.reciprocal(rsm[u][:], rsm[u][:]))
                    for q in range(2):
                        rows = slice(q * K, (q + 1) * K)
                        V.tensor_tensor(S[u][rows, :, rows], ex[u][rows],
                                        bc(rsm[u][rows], 2, [K, GT, K]), ALU.mult).then_inc(soft_sb, 1)
                for u in U2:
                    dve.wait_ge(y1_b, n[u])
                    V.scalar_tensor_tensor(y1T[u][:], yb[u][:], 0.01, yb[u][:], ALU.mult, ALU.max).then_inc(y1_sb, 1)
                for u in U2:
                    dve.wait_ge(y2_b, n[u])
                    V.scalar_tensor_tensor(y2T[u][:], yb[u][:], 0.01, yb[u][:], ALU.mult, ALU.max).then_inc(y2_sb, 1)
                for u in U2:
                    dve.wait_ge(z_ps, n[u])
                    normalise(link, lambda t: BANKS[u][1][:, t * D:(t + 1) * D], st6[u], mv[u], var_z)
                for u in U2:
                    dve.wait_ge(rstd_z, n[u])
                    for t in range(GT):
                        V.tensor_scalar(zn[u][:, t, :], BANKS[u][1][:, t * D:(t + 1) * D], mv[u][:, t, 0:1],
                                        rstd[u][:, t:t + 1], ALU.subtract, ALU.mult).then_inc(zn_sb, 1)
                for u in U2:
                    dve.wait_ge(r_sb[u], it + 2)
                    normalise(link, lambda t: zn[u][:, t, :], st6[u], mv[u], var_r)
                for u in U2:
                    dve.wait_ge(rstd_r, n[u])
                    dve.wait_ge(stored[u], 3 * 16 * it + 1)
                    for t in range(GT):
                        V.tensor_scalar(x1[u][:, t, :], zn[u][:, t, :], mv[u][:, t, 0:1],
                                        rstd[u][:, t:t + 1], ALU.subtract, ALU.mult).then_inc(x1_sb[u], 1)
                assert steps[0] == DVE0, steps

            def batch(b):
                link, steps = chain(dve, dve_b, b * DVE_B)
                dve.wait_ge(hb_in, 2 * 16 * (b + 1))
                V.reduce_max(rm[:], hb[:, :, D:HR].rearrange("p t h -> p h t"), AX_X).then_inc(rm_sb, 1)
                dve.wait_ge(rmT_ps, b + 1)
                link(V.reduce_max(R4[:], RHO[0][0:H, 0:P], AX_X))
                V.tensor_scalar(diagR[:], ident[0:H, 0:H], R4[:], None, ALU.mult).then_inc(diag_sb, 1)
                link(V.tensor_tensor(R4W[:], R4[:], we_s[0:H, 7:8], ALU.add))
                V.tensor_scalar(left[:], left[:], R4W[:], -100.0, ALU.add, ALU.max).then_inc(left_sb, 1)
                dve.wait_ge(Rb_ps, b + 1)
                link(V.tensor_copy(Rb[:], RHO[1][:, 0:H]))
                V.tensor_tensor(sig[:], hb[:, :, D:HR], bc(Rb[:], 1, [P, JT, H]), ALU.subtract).then_inc(sig_sb, 1)
                dve.wait_ge(sv_sb, 2 * (b + 1))
                dve.wait_ge(pv_done, JT * NB * b)
                V.tensor_tensor(haug[:, :, :, 0:DH], hb[:, :, 0:D].rearrange("p t (h d) -> p t h d", h=H),
                                bc(v_j[:], 3, [P, JT, H, DH]), ALU.mult).then_inc(haug_sb, 1)
                V.tensor_copy(haug[:, :, :, DH], v_j[:]).then_inc(haug_sb, 1)
                assert steps[0] == DVE_B, steps

            def tile(b, g, ib, k, crossing):
                m = JT * g + k
                slot = X[k % NX]
                dve.wait_ge(F_sb, m + 1)
                if not (isinstance(g, int) and g == 0 and k < NX):
                    dve.wait_ge(pv_done, m - NX + 1)
                for h in range(H):
                    if k == 0:
                        dve.wait_ge(rho_ps, H * g + h + 1)
                    V.scalar_tensor_tensor(slot[:, h, :], F[k % NF][:], s_j[:, k, h:h + 1], RHO[h],
                                           ALU.mult, ALU.max).then_inc(X_sb, 1)
                dve.wait_ge(E_sb, m + 1)
                dve.wait_ge(X_sb, H * (m + 1))
                V.tensor_tensor(slot[:, H - 1, :], slot[:, H - 1, :], E[k % NF][:], ALU.mult).then_inc(P_dve, 1)

            def epilogue(g, k):
                if k == 5:
                    link, steps = chain(dve, dve_e, g * DVE_E)
                    dve.wait_ge(nat_sb, 2 * (g + 1))
                    parts = natO[:].rearrange("p r t (a d) -> p r t a d", a=2)
                    link(V.reciprocal(rden[:], parts[:, :, :, :, DH]))
                    heads = res[:].rearrange("p t (r a d) -> p r t a d", r=2, a=2)
                    for r in range(2):
                        V.tensor_tensor(heads[:, r], parts[:, r, :, :, 0:DH], bc(rden[:, r], 3, [P, GT, 2, DH]),
                                        ALU.mult).then_inc(res_sb, 1)
                    dve.wait_ge(res_sb, 2 * (g + 1) + 1)
                    dve.wait_ge(x1_in, 16 * (g + 1))
                    link(V.tensor_tensor(res[:], res[:], x1b[:], ALU.add))
                    link(V.tensor_tensor(res[:], res[:], bc(bias_bc[:], 1, [P, GT, D]), ALU.add))
                    link(V.scalar_tensor_tensor(lky[:], res[:], 0.5, res[:], ALU.mult, ALU.max))
                    link(V.tensor_tensor(lky[:], lky[:], x1b[:], ALU.add))
                    normalise(link, lambda t: lky[:, t, :], est6, emv, evar)
                    assert steps[0] == DVE_E, steps
                if k == 7:
                    dve.wait_ge(erstd_sb, g + 1)
                    dve.wait_ge(out_st, 16 * g + 1)
                    for t in range(GT):
                        V.tensor_scalar(o_sb[:, t, :], lky[:, t, :], emv[:, t, 0:1], erstd[:, t:t + 1],
                                        ALU.subtract, ALU.mult).then_inc(o_done, 1)

            walk(dve, batch, tile, epilogue)

        @block.tensor
        def _(pe):
            T = nc.tensor

            def mm(o, l, r, start=True, stop=True):
                return T.matmul(o, l, r, start=start, stop=stop)

            pe.wait_ge(weights_in, 16 * N_WEIGHTS)
            pe.wait_ge(const_set, N_CONST)
            T.transpose(bank[0][:, 0:D], W_sb[:, 0:D], ident[:]).then_inc(prep_pe, 1)
            T.transpose(bank[1][:, 0:D], Wp_sb[:], ident[:]).then_inc(prep_pe, 1)
            mm(bank[2][:, 0:2 * H], Wp_sb[:], wlr[:]).then_inc(prep_pe, 1)
            pe.wait_ge(prep_act, 1)
            mm(bank[3][:, 0:1], WT[:], a_sb[:]).then_inc(prep_pe, 1)
            pe.wait_ge(prep_act, 5)

            def tsl(t):
                return slice(t * P, (t + 1) * P)

            with pe.Fori(0, NG // 2) as it:
                n = [2 * it + u + 1 for u in U2]
                for u in U2:
                    pe.wait_ge(x_in[u], 3 * 16 * (it + 1))
                    pe.wait_ge(h_sb[u], 3 * it + 1)
                    for t in range(GT):
                        ins = T.transpose(BANKS[u][0][:, tsl(t)], xg[u][:, t, :], ident[:])
                    ins.then_inc(xT_ps, 1)
                for u in U2:
                    pe.wait_ge(xT_sb, n[u])
                    for t in range(GT):
                        at = (t % 2) * (D + 1)
                        ins = mm(BANKS[u][1 + t // 2][:, at:at + D + 1], xT[u][:, tsl(t)], W_sb[:])
                    ins.then_inc(wh_ps, 1)
                for u in U2:
                    pe.wait_ge(soft_sb, 2 * n[u])
                    for t in range(GT):
                        ins = T.transpose(BANKS[u][0][:, tsl(t)], S[u][:, t, :], ident[:])
                    ins.then_inc(ST_ps, 1)
                for u in U2:
                    pe.wait_ge(ST_sb, n[u])
                    for t in range(GT):
                        ins = mm(BANKS[u][3][:, tsl(t)], whe[u][:, t, 0:D], ST[u][:, tsl(t)])
                    ins.then_inc(oT_ps, 1)
                for u in U2:
                    pe.wait_ge(oT_sb, n[u])
                    mm(BANKS[u][0], W1_sb[:], oT[u][:]).then_inc(y1_ps, 1)
                for u in U2:
                    pe.wait_ge(y1_sb, n[u])
                    mm(BANKS[u][3], W2_sb[:], y1T[u][:]).then_inc(y2_ps, 1)
                for u in U2:
                    pe.wait_ge(y2_sb, n[u])
                    for t in range(GT):
                        z = BANKS[u][1][:, tsl(t)]
                        mm(z, y2T[u][:, tsl(t)], W3_sb[:], stop=False)
                        mm(z, ST[u][:, tsl(t)], whe[u][:, t, 0:D], start=False, stop=False)
                        ins = mm(z, ones_row[0:1, 0:P], b3_row[:], start=False)
                    ins.then_inc(z_ps, 1)
                for u in U2:
                    pe.wait_ge(x1_sb[u], GT * (it + 1))
                    for t in range(GT):
                        ins = T.transpose(BANKS[u][2][:, tsl(t)], x1[u][:, t, :], ident[:])
                    ins.then_inc(x1T_ps, 1)
                for u in U2:
                    pe.wait_ge(x1T_sb, n[u])
                    mm(BANKS[u][0][0:H, :], Wsl[:], x1T[u][:])
                    for t in range(GT):
                        at = (t % 2) * HR
                        ins = mm(BANKS[u][1 + t // 2 * 2][:, at:at + HR], x1T[u][:, tsl(t)], WpT[:])
                    ins.then_inc(h_ps, 1)

            for u in U2:
                pe.wait_ge(h_sb[u], 3 * (NG // 2) + 1)
            pe.wait_ge(prep_dve, 11)

            def transpose_adj(g, k):
                m = JT * g + k
                c = k // CHUNK
                pe.wait_ge(pen_sb, m + 1)
                if isinstance(g, int) and g == 0:
                    if k >= 2:
                        pe.wait_ge(E_sb, m - 1)
                elif k in (4, 5):
                    pe.wait_ge(nat_sb, 2 * g + k - 5)
                else:
                    pe.wait_ge(E_sb, m - 1)
                for t in range(GT):
                    o = TA[k % 2][:, tsl(t)]
                    a0 = (k % CHUNK) * P
                    T.matmul(o, adj_sb[c][:, t, a0:a0 + P], ident[:], is_transpose=True, start=True, stop=False)
                    ins = mm(o, pen[k % NPEN][:, t, :], sgn_ident[:], start=False)
                ins.then_inc(adjT_ps, 1)

            def rho(g, ib):
                for h in range(H):
                    if not (isinstance(g, int) and g == 0):
                        pe.wait_ge(X_sb, JT * H * g - H + h + 1)
                    mm(RHO[h], sel[:, h, :], rho4[:, bass.ts(ib, GROUP)]).then_inc(rho_ps, 1)

            for k in range(LAG):
                transpose_adj(0, k)

            def batch(b):
                pe.wait_ge(rm_sb, b + 1)
                if not isinstance(b, int):
                    pe.wait_ge(X_sb, H * JT * NB * b)
                T.transpose(RHO[0][0:H, 0:P], rm[:], ident[:]).then_inc(rmT_ps, 1)
                pe.wait_ge(diag_sb, b + 1)
                mm(RHO[1][:, 0:H], ones[:], diagR[:]).then_inc(Rb_ps, 1)
                for t in range(JT):
                    ins = mm(RHO[2][0:1, 0:D], tiny[:], hb[:, t, 0:D], start=(t == 0), stop=(t == JT - 1))
                ins.then_inc(hsum_ps, 1)
                pe.wait_ge(rho_sb, b + 1)
                pe.wait_ge(sig_sb, b + 1)
                pe.wait_ge(hmean_sb, b + 1)
                rho(b * NB, 0)
                pe.wait_ge(haug_sb, 2 * (b + 1))

            def tile(b, g, ib, k, crossing):
                m = JT * g + k
                if k + LAG < JT:
                    transpose_adj(g, k + LAG)
                elif not is_last(g):
                    transpose_adj(g + 1, k + LAG - JT)
                if k == JT - 1 and not crossing and not is_last(g):
                    rho(g + 1, ib + 1)
                if k == 0:
                    if not (isinstance(g, int) and g == 0):
                        pe.wait_ge(accU_sb, 2 * g)
                    for h in range(H):
                        rows = slice(64 * (h % 2), 64 * (h % 2) + HA)
                        mm(ACC[h // 2][rows, :], hmean[:, h, :], ones_row[:], stop=False)
                pe.wait_ge(P_pool, m + 1)
                for h in range(H):
                    if h == H - 1:
                        pe.wait_ge(P_dve, m + 1)
                    rows = slice(64 * (h % 2), 64 * (h % 2) + HA)
                    ins = mm(ACC[h // 2][rows, :], haug[:, k, h, :], X[k % NX][:, h, :], start=False, stop=(k == JT - 1))
                ins.then_inc(pv_done, 1)

            def epilogue(g, k):
                if k == 1:
                    pe.wait_ge(accU_sb, 2 * (g + 1))
                    for r in range(2):
                        if is_last(g):
                            pe.wait_ge(E_sb, JT * NG)
                        else:
                            pe.wait_ge(E_sb, JT * (g + 1) + 3 + r)
                        for t in range(GT):
                            ins = T.transpose(TA[r][:, tsl(t)], accU[:, r, tsl(t)], ident[:])
                        ins.then_inc(nat_ps, 1)

            walk(pe, batch, tile, epilogue)


_INS = ['x', 'adj', 'L0_gnn_W', 'L0_gnn_a', 'L0_gnn_ln_g', 'L0_gnn_ln_b', 'L0_gnn_W1', 'L0_gnn_b1', 'L0_gnn_W2',
        'L0_gnn_b2', 'L0_gnn_W3', 'L0_gnn_b3', 'L1_gnn_W_proj', 'L1_gnn_a_w', 'L1_gnn_bias']


def kernel(**inputs):
    import numpy as _np
    import concourse.bacc as _bacc
    from concourse import mybir as _mybir
    from concourse.bass_utils import run_bass_kernel_spmd as _run

    nc = _bacc.Bacc("TRN2", target_bir_lowering=False, num_devices=1)
    arrays, args = {}, []
    for name in _INS:
        a = _np.ascontiguousarray(inputs[name])
        arrays[f"in_{name}_dram"] = a
        args.append(nc.dram_tensor(f"in_{name}_dram", a.shape, _mybir.dt.from_np(a.dtype), kind="ExternalInput").ap())
    shape = tuple(inputs['x'].shape)
    args.append(nc.dram_tensor("out_0_dram", shape, _mybir.dt.float32, kind="ExternalOutput").ap())
    build_program(nc, *args)
    r = _run(nc, [arrays], core_ids=[0])
    return r.results[0]["out_0_dram"]
```

```python
import concourse.bass as bass
from concourse import mybir
from contextlib import ExitStack


def build_program(nc, x, adj, W, a, ln_g, ln_b, W1, b1, W2, b2, W3, b3, W_proj, a_w, bias, out):
    fp32 = mybir.dt.float32
    bf16 = mybir.dt.bfloat16
    ALU = mybir.AluOpType
    ACT = mybir.ActivationFunctionType
    AX_X = mybir.AxisListType.X

    B, N, D = x.shape
    P = 128
    DH = (a_w.shape[1] - 1) // 2
    H = D // DH
    K = 64
    GT = 4
    GROUP = GT * P
    NB = N // GROUP
    NG = B * NB
    JT = N // P
    HA = DH + 1
    HR = D + 2 * H
    CHUNK = 4
    NC_ = JT // CHUNK
    EPS = 1e-5
    PAD = 1.0000001111620804e-05
    BIG = 2.0 ** 100
    TINY = 1e-30
    LAG = 3
    CUT = 24 * GROUP // 32

    x1_d = nc.dram_tensor("x1_scratch", [NG, P, GT * D], fp32).ap()
    h_d = nc.dram_tensor("h_scratch", [NG, P, GT * HR], fp32).ap()
    rho_d = nc.dram_tensor("rho_scratch", [B, H * JT, P], fp32).ap()

    x_g = x.rearrange("b (g t p) f -> (b g) p t f", p=P, t=GT)
    out_g = out.rearrange("b (g t p) f -> (b g) p t f", p=P, t=GT)
    h_b = h_d.rearrange("(b g) p c -> b p g c", g=NB)
    rho_b = rho_d.rearrange("b (h g t) i -> b g h (t i)", h=H, g=NB)
    adj_g = adj.rearrange("b (g t p) j -> (b g) p t j", p=P, t=GT)

    ctx = ExitStack()
    with ctx:
        def sb(name, shape, dt=fp32):
            return ctx.enter_context(nc.sbuf_tensor(name, shape, dt))

        def sem(name):
            return ctx.enter_context(nc.semaphore(name))

        def bc(ap, axis, shape):
            return ap.unsqueeze(axis).broadcast_to(shape)

        ident = sb("ident", [P, P])
        ones = sb("ones", [H, P])
        ones_row = sb("ones_row", [1, GROUP])
        tiny = sb("tiny", [P, 1])
        zero = sb("zero", [P, GT])
        mhalf = sb("mhalf", [P, GT])
        eps_c = sb("eps_c", [P, GT])
        pen_bias = sb("pen_bias", [P, 1])
        sgn_ident = sb("sgn_ident", [P, P], bf16)
        we_raw = sb("we_raw", [P, 1])
        we_s = sb("we_s", [P, 8])
        W_sb = sb("W_sb", [P, D + 1])
        WT = sb("WT", [P, D])
        a_sb = sb("a_sb", [P, 1])
        W1_sb = sb("W1_sb", [P, D])
        W2_sb = sb("W2_sb", [P, D])
        W3_sb = sb("W3_sb", [P, D])
        b1_sb = sb("b1_sb", [P, 1])
        b2_sb = sb("b2_sb", [P, 1])
        b3_row = sb("b3_row", [1, D])
        g_bc = sb("g_bc", [P, D])
        b_bc = sb("b_bc", [P, D])
        bias_bc = sb("bias_bc", [P, D])
        Wp_sb = sb("Wp_sb", [P, D])
        WpT = sb("WpT", [P, HR])
        wlr = sb("wlr", [P, 2 * H])

        NX = 4
        X = [sb(f"X{r}", [P, H, GROUP]) for r in range(NX)]

        U = range(NB)
        assert NB == NX
        ST = [X[u][:, 0, :] for u in U]
        act_T = [X[u][:, 1, :] for u in U]
        yb = [X[u][:, 2, :] for u in U]
        zn = [yb[u].rearrange("p (t f) -> p t f", t=GT) for u in U]
        xg = [X[u][:, 3, :].rearrange("p (t f) -> p t f", t=GT) for u in U]
        blk = [sb(f"blk{u}", [P, GT, K]) for u in U]
        wh_h = [sb(f"wh_h{u}", [P, GT, HR]) for u in U]
        e_l = [sb(f"e_l{u}", [P, GT]) for u in U]
        ex = [sb(f"ex{u}", [P, GT, K]) for u in U]
        rmx = [sb(f"rmx{u}", [P, GT]) for u in U]
        rsm = [sb(f"rsm{u}", [P, GT]) for u in U]
        S = [sb(f"S{u}", [P, GT, P]) for u in U]
        st6 = [sb(f"st6{u}", [P, GT, 6]) for u in U]
        mv = [sb(f"mv{u}", [P, GT, 2]) for u in U]
        ve = [sb(f"ve{u}", [P, GT]) for u in U]
        rstd = [sb(f"rstd{u}", [P, GT]) for u in U]

        NG_ = 4
        NE = 4
        NPEN = 4
        adj_sb = [sb(f"adj_sb{c}", [P, GT, CHUNK * P]) for c in range(NC_)]
        pen = [sb(f"pen{r}", [P, GT, P], bf16) for r in range(NPEN)]
        E = [sb(f"E{r}", [P, GROUP]) for r in range(NE)]
        G = [sb(f"G{r}", [P, GROUP]) for r in range(NG_)]
        RHO = sb("RHO", [P, 2, H, GROUP])
        hb = sb("hb", [P, JT, HR])
        lam = sb("lam", [P, JT, H])
        rho_n = sb("rho_n", [P, H * JT])
        rho_T = sb("rho_T", [H * JT, P])
        rm = sb("rm", [P, H])
        R4 = sb("R4", [H, 1])
        diagR = sb("diagR", [H, H])
        Rb = sb("Rb", [P, H])
        sig = sb("sig", [P, JT, H])
        s_next = sb("s_next", [P, JT, H])
        s_j = sb("s_j", [P, JT, H])
        v_j = sb("v_j", [P, JT, H])
        haug = sb("haug", [P, JT, H, HA])
        hmean = sb("hmean", [1, H, HA])
        accU = sb("accU", [P, 2, GROUP])
        natO = sb("natO", [P, 2, GT, P])
        rden = sb("rden", [P, 2, GT, 2])
        x1b = sb("x1b", [P, GT, D])
        xbias = sb("xbias", [P, GT, D])
        res = sb("res", [P, GT, D])
        lky = sb("lky", [P, GT, D])
        est6 = sb("est6", [P, GT, 6])
        emv = sb("emv", [P, GT, 2])
        eve = sb("eve", [P, GT])
        erstd = sb("erstd", [P, GT])
        eprod = sb("eprod", [P, GT])
        eshift = sb("eshift", [P, GT])
        o_sb = sb("o_sb", [P, GT, D])

        psum = ctx.enter_context(nc.psum_tensor("psum", [P, 8, GROUP], fp32))
        bank = [psum[:, i, :] for i in range(8)]
        BA = bank[0:4]
        BB = bank[4:8]
        TA = bank[0:4]
        NT = len(TA)
        LB = bank[4:6]
        ACC = bank[6:8]

        const_set = sem("const_set")
        weights_in = sem("weights_in")
        prep_pe = sem("prep_pe")
        prep_dve = sem("prep_dve")
        prep_act = sem("prep_act")
        x_in = [sem(f"x_in{u}") for u in U]
        xT_ps = sem("xT_ps")
        xT_sb = sem("xT_sb")
        wh_ps = sem("wh_ps")
        wh_sb = sem("wh_sb")
        xb_sb = sem("xb_sb")
        scores_sb = sem("scores_sb")
        exp_sb = sem("exp_sb")
        soft_sb = sem("soft_sb")
        ST_ps = sem("ST_ps")
        ST_sb = sem("ST_sb")
        oT_ps = sem("oT_ps")
        oT_sb = sem("oT_sb")
        y1_ps = sem("y1_ps")
        y1_b = sem("y1_b")
        y1_sb = sem("y1_sb")
        y2_ps = sem("y2_ps")
        y2_b = sem("y2_b")
        y2_sb = sem("y2_sb")
        z_ps = sem("z_ps")
        var_z = sem("var_z")
        rstd_z = sem("rstd_z")
        zn_sb = sem("zn_sb")
        r_sb = [sem(f"r_sb{u}") for u in U]
        var_r = sem("var_r")
        rstd_r = sem("rstd_r")
        x1_sb = [sem(f"x1_sb{u}") for u in U]
        x1T_ps = sem("x1T_ps")
        x1T_sb = sem("x1T_sb")
        h_ps = sem("h_ps")
        h_sb = [sem(f"h_sb{u}") for u in U]
        stored = [sem(f"stored{u}") for u in U]
        dve0 = sem("dve0")
        pool0 = sem("pool0")
        adj_in = [sem(f"adj_in{c}") for c in range(NC_)]
        pen_sb = sem("pen_sb")
        adjT_ps = sem("adjT_ps")
        G_sb = sem("G_sb")
        E_sb = sem("E_sb")
        B_pool = sem("B_pool")
        B_dve = sem("B_dve")
        X_sb = sem("X_sb")
        pv_done = sem("pv_done")
        rho_st = sem("rho_st")
        rho_in = sem("rho_in")
        s_sb = sem("s_sb")
        shift_sb = sem("shift_sb")
        accU_sb = sem("accU_sb")
        nat_ps = sem("nat_ps")
        nat_sb = sem("nat_sb")
        hb_in = sem("hb_in")
        rm_sb = sem("rm_sb")
        rmT_ps = sem("rmT_ps")
        diag_sb = sem("diag_sb")
        Rb_ps = sem("Rb_ps")
        sig_sb = sem("sig_sb")
        sv_sb = sem("sv_sb")
        lam_sb = sem("lam_sb")
        rho_n_sb = sem("rho_n_sb")
        rho_ps = sem("rho_ps")
        rho_sb = sem("rho_sb")
        hv_sb = sem("hv_sb")
        haug_sb = sem("haug_sb")
        hsum_ps = sem("hsum_ps")
        hmean_sb = sem("hmean_sb")
        res_sb = sem("res_sb")
        x1_in = sem("x1_in")
        xbias_sb = sem("xbias_sb")
        evar = sem("evar")
        erstd_sb = sem("erstd_sb")
        o_done = sem("o_done")
        out_st = sem("out_st")
        dve_b = sem("dve_b")
        dve_e = sem("dve_e")
        pool_turn = sem("pool_turn")
        pool_e = sem("pool_e")

        N_WEIGHTS = 13 + 2 * H
        N_CONST = 15
        POOL0, DVE0, DVE_B, DVE_E, POOL_E = 16, 20, 3, 4, 3

        def chain(eng, semaphore, base):
            count = [0]

            def link(ins):
                count[0] += 1
                ins.then_inc(semaphore, 1)
                eng.wait_ge(semaphore, base + count[0])
            return link, count

        HEAD = 8

        def walk(eng, prepare, tile, epilogue):
            def step(b, g, ib, crossing):
                for k in range(HEAD, JT):
                    if crossing:
                        prepare(b + 1, k)
                    tile(b, g, ib, k, crossing)
                for k in range(HEAD):
                    tile(b + 1 if crossing else b, g + 1, 0 if crossing else ib + 1, k, crossing)
                    epilogue(g, k)

            for k in range(HEAD, JT):
                prepare(0, k)
            for k in range(HEAD):
                tile(0, 0, 0, k, True)
            with eng.Fori(0, B - 1) as b:
                with eng.Fori(0, NB - 1) as ib:
                    step(b, b * NB + ib, ib, False)
                step(b, b * NB + (NB - 1), NB - 1, True)
            with eng.Fori(0, NB - 1) as ib:
                step(B - 1, ib + (B - 1) * NB, ib, False)
            for k in range(HEAD, JT):
                tile(B - 1, NG - 1, NB - 1, k, False)
            for k in range(HEAD):
                epilogue(NG - 1, k)

        def is_last(g):
            return isinstance(g, int) and g == NG - 1

        block = ctx.enter_context(nc.Block())

        @block.sync
        def _(sp):
            for dst, src in ((W_sb[:, 0:D], W), (a_sb[:], a), (W1_sb[:], W1), (W2_sb[:], W2), (W3_sb[:], W3),
                             (b1_sb[:], b1.unsqueeze(1)), (b2_sb[:], b2.unsqueeze(1)), (b3_row[:], b3.unsqueeze(0)),
                             (g_bc[:], ln_g.partition_broadcast(P)), (b_bc[:], ln_b.partition_broadcast(P)),
                             (bias_bc[:], bias.partition_broadcast(P)), (Wp_sb[:], W_proj),
                             (we_raw[:], a_w[0, 2 * DH:2 * DH + 1].partition_broadcast(P))):
                sp.dma_start(dst, src).then_inc(weights_in, 16)
            sp.wait_ge(const_set, 1)
            for h in range(H):
                for side in range(2):
                    sp.dma_start(wlr[h * DH:(h + 1) * DH, (1 - side) * H + h:(1 - side) * H + h + 1],
                                 a_w[0, side * DH:(side + 1) * DH].unsqueeze(1)).then_inc(weights_in, 16)

            sp.sem_inc(res_sb, 1)
            sp.sem_inc(out_st, 1)
            for u in U:
                sp.sem_inc(r_sb[u], 1)
                sp.sem_inc(h_sb[u], 1)
                sp.sem_inc(stored[u], 1)

            with sp.Fori(0, B) as b:
                for u in U:
                    sp.wait_ge(r_sb[u], b + 1)
                    sp.dma_start(xg[u], x_g[b * NB + u]).then_inc(x_in[u], 16)
                    for q in range(2):
                        at = b * (N * N) + (u * GROUP + q * K) * (N + 1)
                        sp.dma_start(blk[u][q * K:(q + 1) * K],
                                     bass.AP(adj.tensor, at, [[N, K], [P * (N + 1), GT], [1, K]])) \
                            .then_inc(x_in[u], 16)

            def load_adj(g, c):
                sp.dma_start(adj_sb[c][:], adj_g[g][:, :, c * CHUNK * P:(c + 1) * CHUNK * P]).then_inc(adj_in[c], 16)

            LOAD_AT = (HEAD, HEAD + 1, HEAD + 4, HEAD + 6)

            def load_batch(b):
                sp.dma_start(hb[:].rearrange("p (g t) c -> p g (t c)", g=NB), h_b[b]).then_inc(hb_in, 16)

            for c in range(NC_):
                load_adj(0, c)
            for u in U:
                sp.wait_ge(stored[u], 2 * 16 * B + 1)
            sp.dma_start(x1b[:], x1_d[0]).then_inc(x1_in, 16)

            def load_rho(b, ib):
                sp.dma_start(RHO[:, ib % 2], rho_b[b][ib].partition_broadcast(P)).then_inc(rho_in, 16)

            def prepare(b, k):
                if k == HEAD:
                    if not (isinstance(b, int) and b == 0):
                        sp.wait_ge(haug_sb, 2 * NC_ * b)
                        sp.wait_ge(hsum_ps, b)
                        sp.wait_ge(lam_sb, b)
                    load_batch(b)
                if k == JT - 2:
                    sp.wait_ge(rho_sb, b + 1)
                    sp.dma_start(rho_d[b], rho_T[:]).then_inc(rho_st, 16)
                    sp.wait_ge(rho_st, 16 * (b + 1))
                    load_rho(b, 0)

            def tile(b, g, ib, k, crossing):
                if k in LOAD_AT and not is_last(g):
                    c = LOAD_AT.index(k)
                    sp.wait_ge(adjT_ps, JT * g + CHUNK * (c + 1))
                    load_adj(g + 1, c)
                if k == HEAD + 2 and not crossing and not is_last(g):
                    if not (isinstance(g, int) and g == 0):
                        sp.wait_ge(B_pool, JT * g + 1)
                        sp.wait_ge(B_dve, JT * g + 1)
                    load_rho(b, ib + 1)

            def epilogue(g, k):
                if k == HEAD - 1:
                    sp.wait_ge(o_done, GT * (g + 1))
                    sp.dma_start(out_g[g], o_sb[:]).then_inc(out_st, 16)
                    if not is_last(g):
                        sp.dma_start(x1b[:], x1_d[g + 1]).then_inc(x1_in, 16)

            walk(sp, prepare, tile, epilogue)
            sp.wait_ge(out_st, 16 * NG + 1)

        @block.gpsimd
        def _(pool):
            nc.gpsimd.memset(wlr[:], 0.0).then_inc(const_set, 1)
            nc.gpsimd.memset(ident[:], 0.0).then_inc(const_set, 1)
            nc.gpsimd.memset(ones[:], 1.0).then_inc(const_set, 1)
            nc.gpsimd.memset(ones_row[:], 1.0).then_inc(const_set, 1)
            nc.gpsimd.memset(tiny[:], TINY).then_inc(const_set, 1)
            nc.gpsimd.memset(mhalf[:], -0.5).then_inc(const_set, 1)
            nc.gpsimd.memset(zero[:], 0.0).then_inc(const_set, 1)
            nc.gpsimd.memset(eps_c[:], EPS).then_inc(const_set, 1)
            nc.gpsimd.memset(hmean[:], N * TINY).then_inc(const_set, 1)
            nc.gpsimd.memset(accU[:], 0.0).then_inc(const_set, 1)
            for u in U:
                nc.gpsimd.memset(S[u][:], 0.0).then_inc(const_set, 1)
            pool.wait_ge(const_set, N_CONST - 1)
            nc.gpsimd.affine_select(out=ident[:], in_=ident[:], compare_op=ALU.not_equal, fill=1.0, base=0,
                                    pattern=[[-1, P]], channel_multiplier=1).then_inc(const_set, 1)

            pool.wait_ge(weights_in, 16 * N_WEIGHTS)
            with pool.Fori(0, B) as b:
                link, steps = chain(pool, pool0, b * POOL0)
                for u in U:
                    pool.wait_ge(xT_ps, NB * b + u + 1)
                    link(nc.gpsimd.tensor_tensor(xg[u], xg[u], bc(b_bc[:], 1, [P, GT, D]), ALU.add))
                for u in U:
                    pool.wait_ge(var_z, GT * (NB * b + u + 1))
                    link(nc.gpsimd.tensor_tensor(ve[u][:], mv[u][:, :, 1], eps_c[:], ALU.add))
                    nc.gpsimd.tensor_tensor(rstd[u][:], ve[u][:], mhalf[:], ALU.pow).then_inc(rstd_z, 1)
                for u in U:
                    pool.wait_ge(zn_sb, GT * (NB * b + u + 1))
                    link(nc.gpsimd.tensor_tensor(zn[u], zn[u], bc(g_bc[:], 1, [P, GT, D]), ALU.mult))
                    nc.gpsimd.tensor_tensor(zn[u], zn[u], xg[u], ALU.add).then_inc(r_sb[u], 1)
                for u in U:
                    pool.wait_ge(var_r, GT * (NB * b + u + 1))
                    link(nc.gpsimd.tensor_tensor(ve[u][:], mv[u][:, :, 1], eps_c[:], ALU.add))
                    nc.gpsimd.tensor_tensor(rstd[u][:], ve[u][:], mhalf[:], ALU.pow).then_inc(rstd_r, 1)
                assert steps[0] == POOL0

            def prepare(b, k):
                pass

            def tile(b, g, ib, k, crossing):
                m = JT * g + k
                if k == 0:
                    pool.wait_ge(rho_in, 16 * (g + 1))
                if not (isinstance(g, int) and g == 0 and k < NX):
                    pool.wait_ge(pv_done, m - NX + 1)
                pool.wait_ge(E_sb, m + 1)
                pool.sem_inc(pool_turn, 1)
                nc.gpsimd.tensor_tensor(X[k % NX][:, :, 0:CUT], RHO[:, ib % 2, :, 0:CUT],
                                        bc(E[k % NE][:, 0:CUT], 1, [P, H, CUT]), ALU.mult).then_inc(B_pool, 1)

            def epilogue(g, k):
                link, steps = chain(pool, pool_e, g * POOL_E)
                if k == 2:
                    pool.wait_ge(x1_in, 16 * (g + 1))
                    nc.gpsimd.tensor_tensor(xbias[:], x1b[:], bc(bias_bc[:], 1, [P, GT, D]),
                                            ALU.add).then_inc(xbias_sb, 1)
                if k == 5:
                    pool.wait_ge(evar, GT * (g + 1))
                    link(nc.gpsimd.tensor_tensor(eve[:], emv[:, :, 1], eps_c[:], ALU.add))
                    link(nc.gpsimd.tensor_tensor(erstd[:], eve[:], mhalf[:], ALU.pow))
                    link(nc.gpsimd.tensor_tensor(eprod[:], emv[:, :, 0], erstd[:], ALU.mult))
                    nc.gpsimd.tensor_tensor(eshift[:], zero[:], eprod[:], ALU.subtract).then_inc(shift_sb, 1)

            walk(pool, prepare, tile, epilogue)

        @block.scalar
        def _(act):
            def copy(dst, src):
                return nc.scalar.activation(dst, src, ACT.Copy)

            act.wait_ge(prep_pe, 1)
            copy(WT[:], bank[0][:, 0:D]).then_inc(prep_act, 1)
            act.wait_ge(prep_pe, 2)
            copy(WpT[:, 0:D], bank[1][:, 0:D]).then_inc(prep_act, 1)
            act.wait_ge(prep_pe, 3)
            copy(WpT[:, D:HR], bank[2][:, 0:2 * H]).then_inc(prep_act, 1)
            act.wait_ge(prep_pe, 4)
            copy(W_sb[:, D:D + 1], bank[3][:, 0:1]).then_inc(prep_act, 1)

            with act.Fori(0, B) as b:
                n = [NB * b + u + 1 for u in U]
                for u in U:
                    act.wait_ge(xT_ps, n[u])
                    copy(act_T[u], BA[u]).then_inc(xT_sb, 1)
                for u in U:
                    act.wait_ge(wh_ps, n[u])
                    act.wait_ge(stored[u], 2 * 16 * b + 1)
                    for half, bk in ((0, BB), (1, BA)):
                        copy(wh_h[u][:, 2 * half:2 * half + 2, 0:D + 1],
                             bk[u][:, 0:2 * (D + 1)].rearrange("p (t c) -> p t c", t=2)).then_inc(wh_sb, 1)
                for u in U:
                    act.wait_ge(scores_sb, n[u])
                    nc.scalar.activation(ex[u][:], ex[u][:], ACT.Exp).then_inc(exp_sb, 1)
                for u in U:
                    act.wait_ge(ST_ps, n[u])
                    copy(ST[u], BB[u]).then_inc(ST_sb, 1)
                for u in U:
                    act.wait_ge(oT_ps, n[u])
                    copy(act_T[u], BA[u]).then_inc(oT_sb, 1)
                for u in U:
                    act.wait_ge(y1_ps, n[u])
                    nc.scalar.activation(yb[u], BB[u], ACT.Identity, bias=b1_sb[:]).then_inc(y1_b, 1)
                for u in U:
                    act.wait_ge(y2_ps, n[u])
                    nc.scalar.activation(yb[u], BA[u], ACT.Identity, bias=b2_sb[:]).then_inc(y2_b, 1)
                for u in U:
                    act.wait_ge(x1_sb[u], GT * (b + 1))
                    act.dma_start(x1_d[NB * b + u], yb[u]).then_inc(stored[u], 16)
                    act.wait_ge(x1T_ps, n[u])
                    copy(act_T[u], BA[u]).then_inc(x1T_sb, 1)
                for u in U:
                    act.wait_ge(h_ps, n[u])
                    for half, bk in ((0, BB), (1, BA)):
                        copy(wh_h[u][:, 2 * half:2 * half + 2, :],
                             bk[u][:, 0:2 * HR].rearrange("p (t c) -> p t c", t=2)).then_inc(h_sb[u], 1)
                for u in U:
                    act.wait_ge(h_sb[u], 2 * b + 3)
                    act.dma_start(h_d[NB * b + u], wh_h[u][:].rearrange("p t c -> p (t c)")).then_inc(stored[u], 16)

            act.wait_ge(prep_dve, 10)

            def penalty(g, k):
                c = k // CHUNK
                act.wait_ge(adj_in[c], 16 * (g + 1))
                if not (isinstance(g, int) and g == 0 and k < NPEN):
                    act.wait_ge(adjT_ps, JT * g + k - NPEN + 1)
                nc.scalar.activation(pen[k % NPEN][:], adj_sb[c][:, :, (k % CHUNK) * P:(k % CHUNK + 1) * P],
                                     ACT.Relu, scale=-BIG, bias=pen_bias[:]).then_inc(pen_sb, 1)

            for k in range(NPEN):
                penalty(0, k)

            def prepare(b, k):
                if k == HEAD + 5:
                    act.wait_ge(lam_sb, b + 1)
                    nc.scalar.activation(rho_n[:].rearrange("p (h t) -> p h t", h=H), lam[:].rearrange("p t h -> p h t"),
                                         ACT.Exp, scale=-0.8).then_inc(rho_n_sb, 1)
                    if not (isinstance(b, int) and b == 0):
                        act.wait_ge(s_sb, b)
                        act.wait_ge(haug_sb, 2 * NC_ * b)
                    act.wait_ge(sig_sb, b + 1)
                    nc.scalar.activation(s_next[:], sig[:], ACT.Exp, scale=0.8).then_inc(sv_sb, 1)
                    nc.scalar.activation(v_j[:], sig[:], ACT.Exp, scale=0.2).then_inc(sv_sb, 1)
                if k == HEAD + 6:
                    act.wait_ge(rho_ps, b + 1)
                    if not (isinstance(b, int) and b == 0):
                        act.wait_ge(rho_st, 16 * b)
                    copy(rho_T[:], LB[0][0:H * JT, 0:P]).then_inc(rho_sb, 1)
                if k == HEAD + 7:
                    act.wait_ge(hsum_ps, b + 1)
                    nc.scalar.activation(hmean[:, :, 0:DH], LB[1][0:1, 0:D].rearrange("p (h d) -> p h d", h=H),
                                         ACT.Copy).then_inc(hmean_sb, 1)

            def tile(b, g, ib, k, crossing):
                m = JT * g + k
                if crossing and 3 <= k < 3 + NC_:
                    if k == 3:
                        act.wait_ge(hv_sb, b + 1)
                    q = slice((k - 3) * CHUNK, (k - 2) * CHUNK)
                    copy(haug[:, q, :, 0:DH], hb[:, q, 0:D].rearrange("p t (h d) -> p t h d", h=H)).then_inc(haug_sb, 1)
                    copy(haug[:, q, :, DH], v_j[:, q]).then_inc(haug_sb, 1)
                act.wait_ge(adjT_ps, m + 1)
                if not (isinstance(g, int) and g == 0 and k < NE):
                    act.wait_ge(B_pool, m - NE + 1)
                    act.wait_ge(B_dve, m - NE + 1)
                nc.scalar.activation(E[k % NE][:], TA[k % NT], ACT.Exp, scale=we_s[:, 3:4],
                                     bias=we_s[:, 5:6]).then_inc(E_sb, 1)
                if not (isinstance(g, int) and g == 0 and k < NG_):
                    act.wait_ge(X_sb, m - NG_ + 1)
                nc.scalar.activation(G[k % NG_][:], TA[k % NT], ACT.Exp, scale=we_s[:, 2:3],
                                     bias=we_s[:, 4:5]).then_inc(G_sb, 1)
                if k + NPEN < JT:
                    penalty(g, k + NPEN)
                elif not is_last(g):
                    penalty(g + 1, k + NPEN - JT)

            def epilogue(g, k):
                if k == 2:
                    act.wait_ge(pv_done, JT * (g + 1))
                    for a_ in range(2):
                        rows = slice(64 * a_, 64 * a_ + HA)
                        copy(accU[rows], psum[rows, 6:8, :]).then_inc(accU_sb, 1)
                if k == 4:
                    act.wait_ge(res_sb, 2 * g + 1)
                    for r in range(2):
                        act.wait_ge(nat_ps, 2 * g + r + 1)
                        copy(natO[:, r].rearrange("p t f -> p (t f)"), LB[r]).then_inc(nat_sb, 1)
                if k == 7:
                    act.wait_ge(shift_sb, g + 1)
                    act.wait_ge(out_st, 16 * g + 1)
                    for t in range(GT):
                        nc.scalar.activation(o_sb[:, t, :], lky[:, t, :], ACT.Identity, scale=erstd[:, t:t + 1],
                                             bias=eshift[:, t:t + 1]).then_inc(o_done, 1)

            walk(act, prepare, tile, epilogue)

        @block.vector
        def _(dve):
            V = nc.vector
            dve.wait_ge(weights_in, 16 * N_WEIGHTS)
            dve.wait_ge(const_set, N_CONST)
            link, _ = chain(dve, prep_dve, 0)
            w = [we_s[:, i:i + 1] for i in range(8)]
            link(V.tensor_scalar(w[0], we_raw[:], 0.0, 2.0, ALU.is_ge, ALU.mult))
            link(V.tensor_scalar(w[0], w[0], -1.0, None, ALU.add))
            link(V.tensor_scalar(w[1], we_raw[:], w[0], 1e-10, ALU.mult, ALU.max))
            link(V.tensor_scalar(w[2], w[1], w[0], None, ALU.mult))
            link(V.tensor_scalar(w[7], w[2], 0.0, None, ALU.max))
            link(V.tensor_scalar(w[3], w[2], 0.2, None, ALU.mult))
            link(V.tensor_scalar(w[4], w[7], -1.0, None, ALU.mult))
            link(V.tensor_scalar(w[5], w[7], -0.2, None, ALU.mult))
            link(V.tensor_scalar(sgn_ident[:], ident[:], w[0], -1.0, ALU.mult, ALU.mult))
            link(V.memset(pen_bias[:], BIG * PAD))

            def normalise(link, src, stats, mean_var, done):
                for t in range(GT):
                    V.bn_stats(stats[:, t, :], src(t))
                dve.drain()
                for t in range(GT):
                    V.bn_aggr(mean_var[:, t, :], stats[:, t, :]).then_inc(done, 1)

            with dve.Fori(0, B) as b:
                link, steps = chain(dve, dve0, b * DVE0)
                n = [NB * b + u + 1 for u in U]
                for u in U:
                    dve.wait_ge(wh_sb, 2 * n[u])
                    wa = wh_h[u][:, :, D]
                    link(V.scalar_tensor_tensor(e_l[u][:], wa, 0.2, wa, ALU.mult, ALU.max))
                    dve.wait_ge(x_in[u], 3 * 16 * (b + 1))
                    link(V.tensor_tensor(ex[u][:], blk[u][:], bc(e_l[u][:], 2, [P, GT, K]), ALU.mult))
                    link(V.reduce_max(rmx[u][:], ex[u][:], AX_X))
                    V.tensor_tensor(ex[u][:], ex[u][:], bc(rmx[u][:], 2, [P, GT, K]),
                                    ALU.subtract).then_inc(scores_sb, 1)
                for u in U:
                    dve.wait_ge(exp_sb, n[u])
                    link(V.reduce_sum(rsm[u][:], ex[u][:], AX_X))
                    link(V.reciprocal(rsm[u][:], rsm[u][:]))
                    for q in range(2):
                        rows = slice(q * K, (q + 1) * K)
                        V.tensor_tensor(S[u][rows, :, rows], ex[u][rows],
                                        bc(rsm[u][rows], 2, [K, GT, K]), ALU.mult).then_inc(soft_sb, 1)
                for u in U:
                    dve.wait_ge(y1_b, n[u])
                    V.scalar_tensor_tensor(act_T[u], yb[u], 0.01, yb[u], ALU.mult, ALU.max).then_inc(y1_sb, 1)
                for u in U:
                    dve.wait_ge(y2_b, n[u])
                    V.scalar_tensor_tensor(act_T[u], yb[u], 0.01, yb[u], ALU.mult, ALU.max).then_inc(y2_sb, 1)
                for u in U:
                    dve.wait_ge(z_ps, n[u])
                    normalise(link, lambda t: BB[u][:, t * D:(t + 1) * D], st6[u], mv[u], var_z)
                for u in U:
                    dve.wait_ge(rstd_z, n[u])
                    for t in range(GT):
                        V.tensor_scalar(zn[u][:, t, :], BB[u][:, t * D:(t + 1) * D], mv[u][:, t, 0:1],
                                        rstd[u][:, t:t + 1], ALU.subtract, ALU.mult).then_inc(zn_sb, 1)
                for u in U:
                    dve.wait_ge(r_sb[u], b + 2)
                    normalise(link, lambda t: zn[u][:, t, :], st6[u], mv[u], var_r)
                for u in U:
                    dve.wait_ge(rstd_r, n[u])
                    for t in range(GT):
                        V.tensor_scalar(zn[u][:, t, :], zn[u][:, t, :], mv[u][:, t, 0:1],
                                        rstd[u][:, t:t + 1], ALU.subtract, ALU.mult).then_inc(x1_sb[u], 1)
                assert steps[0] == DVE0, steps

            def prepare(b, k):
                link, steps = chain(dve, dve_b, b * DVE_B)
                if k == HEAD + 1:
                    dve.wait_ge(hb_in, 16 * (b + 1))
                    V.reduce_max(rm[:], hb[:, :, D:D + H].rearrange("p t h -> p h t"), AX_X).then_inc(rm_sb, 1)
                if k == HEAD + 2:
                    dve.wait_ge(rmT_ps, b + 1)
                    link(V.reduce_max(R4[:], LB[0][0:H, 0:P], AX_X))
                    V.tensor_scalar(diagR[:], ident[0:H, 0:H], R4[:], None, ALU.mult).then_inc(diag_sb, 1)
                if k == HEAD + 3:
                    steps[0] = 1
                    dve.wait_ge(Rb_ps, b + 1)
                    link(V.tensor_copy(Rb[:], LB[0][:, 0:H]))
                    link(V.tensor_tensor(lam[:], hb[:, :, D + H:HR], bc(Rb[:], 1, [P, JT, H]), ALU.add))
                    V.tensor_scalar(lam[:], lam[:], we_s[:, 7:8], -100.0, ALU.add, ALU.max).then_inc(lam_sb, 1)
                    V.tensor_tensor(sig[:], hb[:, :, D:D + H], bc(Rb[:], 1, [P, JT, H]),
                                    ALU.subtract).then_inc(sig_sb, 1)
                if k == HEAD + 6:
                    dve.wait_ge(hsum_ps, b + 1)
                    dve.wait_ge(sv_sb, 2 * (b + 1))
                    h_rows = hb[:, :, 0:D].rearrange("p t (h d) -> p t h d", h=H)
                    V.tensor_tensor(h_rows, h_rows, bc(v_j[:], 3, [P, JT, H, DH]), ALU.mult).then_inc(hv_sb, 1)

            def tile(b, g, ib, k, crossing):
                m = JT * g + k
                slot = X[k % NX]
                if k == 0:
                    dve.wait_ge(rho_in, 16 * (g + 1))
                    if crossing:
                        dve.wait_ge(sv_sb, 2 * (b + 1))
                        if not (isinstance(g, int) and g == 0):
                            dve.wait_ge(X_sb, m)
                        V.tensor_copy(s_j[:], s_next[:]).then_inc(s_sb, 1)
                        dve.wait_ge(s_sb, b + 1)
                if not (isinstance(g, int) and g == 0 and k < NX):
                    dve.wait_ge(pv_done, m - NX + 1)
                dve.wait_ge(E_sb, m + 1)
                V.tensor_tensor(slot[:, :, CUT:], RHO[:, ib % 2, :, CUT:],
                                bc(E[k % NE][:, CUT:], 1, [P, H, GROUP - CUT]), ALU.mult).then_inc(B_dve, 1)
                dve.wait_ge(G_sb, m + 1)
                dve.wait_ge(B_dve, m + 1)
                dve.wait_ge(B_pool, m + 1)
                for h in range(H):
                    ins = V.scalar_tensor_tensor(slot[:, h, :], G[k % NG_][:], s_j[:, k, h:h + 1], slot[:, h, :],
                                                 ALU.mult, ALU.max)
                ins.then_inc(X_sb, 1)

            def epilogue(g, k):
                if k == 3:
                    link, steps = chain(dve, dve_e, g * DVE_E)
                    dve.wait_ge(nat_sb, 2 * (g + 1))
                    parts = natO[:].rearrange("p r t (a d) -> p r t a d", a=2)
                    link(V.reciprocal(rden[:], parts[:, :, :, :, DH]))
                    heads = res[:].rearrange("p t (r a d) -> p r t a d", r=2, a=2)
                    for r in range(2):
                        V.tensor_tensor(heads[:, r], parts[:, r, :, :, 0:DH], bc(rden[:, r], 3, [P, GT, 2, DH]),
                                        ALU.mult).then_inc(res_sb, 1)
                    dve.wait_ge(res_sb, 2 * (g + 1) + 1)
                    dve.wait_ge(xbias_sb, g + 1)
                    link(V.tensor_tensor(res[:], res[:], xbias[:], ALU.add))
                    link(V.scalar_tensor_tensor(lky[:], res[:], 0.5, res[:], ALU.mult, ALU.max))
                    link(V.tensor_tensor(lky[:], lky[:], x1b[:], ALU.add))
                    normalise(link, lambda t: lky[:, t, :], est6, emv, evar)
                    assert steps[0] == DVE_E, steps

            walk(dve, prepare, tile, epilogue)

        @block.tensor
        def _(pe):
            T = nc.tensor

            def mm(o, l, r, start=True, stop=True):
                return T.matmul(o, l, r, start=start, stop=stop)

            pe.wait_ge(weights_in, 16 * N_WEIGHTS)
            pe.wait_ge(const_set, N_CONST)
            T.transpose(bank[0][:, 0:D], W_sb[:, 0:D], ident[:]).then_inc(prep_pe, 1)
            T.transpose(bank[1][:, 0:D], Wp_sb[:], ident[:]).then_inc(prep_pe, 1)
            mm(bank[2][:, 0:2 * H], Wp_sb[:], wlr[:]).then_inc(prep_pe, 1)
            pe.wait_ge(prep_act, 1)
            mm(bank[3][:, 0:1], WT[:], a_sb[:]).then_inc(prep_pe, 1)
            pe.wait_ge(prep_act, 4)

            def tsl(t):
                return slice(t * P, (t + 1) * P)

            with pe.Fori(0, B) as b:
                n = [NB * b + u + 1 for u in U]
                for u in U:
                    pe.wait_ge(x_in[u], 3 * 16 * (b + 1))
                    pe.wait_ge(h_sb[u], 2 * b + 1)
                    for t in range(GT):
                        ins = T.transpose(BA[u][:, tsl(t)], xg[u][:, t, :], ident[:])
                    ins.then_inc(xT_ps, 1)
                for u in U:
                    pe.wait_ge(xT_sb, n[u])
                    for t in range(GT):
                        at = (t % 2) * (D + 1)
                        ins = mm((BB, BA)[t // 2][u][:, at:at + D + 1], act_T[u][:, tsl(t)], W_sb[:])
                    ins.then_inc(wh_ps, 1)
                for u in U:
                    pe.wait_ge(soft_sb, 2 * n[u])
                    for t in range(GT):
                        ins = T.transpose(BB[u][:, tsl(t)], S[u][:, t, :], ident[:])
                    ins.then_inc(ST_ps, 1)
                for u in U:
                    pe.wait_ge(ST_sb, n[u])
                    for t in range(GT):
                        ins = mm(BA[u][:, tsl(t)], wh_h[u][:, t, 0:D], ST[u][:, tsl(t)])
                    ins.then_inc(oT_ps, 1)
                for u in U:
                    pe.wait_ge(oT_sb, n[u])
                    mm(BB[u], W1_sb[:], act_T[u]).then_inc(y1_ps, 1)
                for u in U:
                    pe.wait_ge(y1_sb, n[u])
                    mm(BA[u], W2_sb[:], act_T[u]).then_inc(y2_ps, 1)
                for u in U:
                    pe.wait_ge(y2_sb, n[u])
                    for t in range(GT):
                        z = BB[u][:, tsl(t)]
                        mm(z, act_T[u][:, tsl(t)], W3_sb[:], stop=False)
                        mm(z, ST[u][:, tsl(t)], wh_h[u][:, t, 0:D], start=False, stop=False)
                        ins = mm(z, ones_row[0:1, 0:P], b3_row[:], start=False)
                    ins.then_inc(z_ps, 1)
                for u in U:
                    pe.wait_ge(x1_sb[u], GT * (b + 1))
                    for t in range(GT):
                        ins = T.transpose(BA[u][:, tsl(t)], zn[u][:, t, :], ident[:])
                    ins.then_inc(x1T_ps, 1)
                for u in U:
                    pe.wait_ge(x1T_sb, n[u])
                    for t in range(GT):
                        at = (t % 2) * HR
                        ins = mm((BB, BA)[t // 2][u][:, at:at + HR], act_T[u][:, tsl(t)], WpT[:])
                    ins.then_inc(h_ps, 1)

            for u in U:
                pe.wait_ge(h_sb[u], 2 * B + 1)
            pe.wait_ge(prep_dve, 10)

            def transpose_adj(g, k):
                m = JT * g + k
                c = k // CHUNK
                pe.wait_ge(pen_sb, m + 1)
                if not (isinstance(g, int) and g == 0 and k < NT):
                    pe.wait_ge(G_sb, m - NT + 1)
                for t in range(GT):
                    o = TA[k % NT][:, tsl(t)]
                    a0 = (k % CHUNK) * P
                    T.matmul(o, adj_sb[c][:, t, a0:a0 + P], ident[:], is_transpose=True, start=True, stop=False)
                    ins = mm(o, pen[k % NPEN][:, t, :], sgn_ident[:], start=False)
                ins.then_inc(adjT_ps, 1)

            for k in range(LAG):
                transpose_adj(0, k)

            def prepare(b, k):
                if k == HEAD + 1:
                    pe.wait_ge(rm_sb, b + 1)
                    T.transpose(LB[0][0:H, 0:P], rm[:], ident[:]).then_inc(rmT_ps, 1)
                if k == HEAD + 2:
                    pe.wait_ge(diag_sb, b + 1)
                    mm(LB[0][:, 0:H], ones[:], diagR[:]).then_inc(Rb_ps, 1)
                if k == HEAD + 3:
                    pe.wait_ge(rho_n_sb, b + 1)
                if HEAD + 1 <= k < HEAD + 5:
                    for t in range(GT):
                        j = (k - HEAD - 1) * GT + t
                        ins = mm(LB[1][0:1, 0:D], tiny[:], hb[:, j, 0:D], start=(j == 0), stop=(j == JT - 1))
                    if j == JT - 1:
                        ins.then_inc(hsum_ps, 1)
                    if k == HEAD + 3:
                        T.transpose(LB[0][0:H * JT, 0:P], rho_n[:], ident[:]).then_inc(rho_ps, 1)

            def tile(b, g, ib, k, crossing):
                m = JT * g + k
                if k + LAG < JT:
                    transpose_adj(g, k + LAG)
                elif not is_last(g):
                    transpose_adj(g + 1, k + LAG - JT)
                if k == 0:
                    if crossing:
                        pe.wait_ge(hmean_sb, b + 1)
                        pe.wait_ge(haug_sb, 2 * NC_ * b + 2)
                    if not (isinstance(g, int) and g == 0):
                        pe.wait_ge(accU_sb, 2 * g)
                    for h in range(H):
                        rows = slice(64 * (h % 2), 64 * (h % 2) + HA)
                        mm(ACC[h // 2][rows, :], hmean[:, h, :], ones_row[:], stop=False)
                if k == CHUNK and crossing:
                    pe.wait_ge(haug_sb, 2 * NC_ * (b + 1))
                pe.wait_ge(X_sb, m + 1)
                for h in range(H):
                    rows = slice(64 * (h % 2), 64 * (h % 2) + HA)
                    ins = mm(ACC[h // 2][rows, :], haug[:, k, h, :], X[k % NX][:, h, :], start=False, stop=(k == JT - 1))
                ins.then_inc(pv_done, 1)

            def epilogue(g, k):
                if k == 0:
                    pe.wait_ge(accU_sb, 2 * (g + 1))
                    for r in range(2):
                        for t in range(GT):
                            ins = T.transpose(LB[r][:, tsl(t)], accU[:, r, tsl(t)], ident[:])
                        ins.then_inc(nat_ps, 1)

            walk(pe, prepare, tile, epilogue)


_INS = ['x', 'adj', 'L0_gnn_W', 'L0_gnn_a', 'L0_gnn_ln_g', 'L0_gnn_ln_b', 'L0_gnn_W1', 'L0_gnn_b1', 'L0_gnn_W2',
        'L0_gnn_b2', 'L0_gnn_W3', 'L0_gnn_b3', 'L1_gnn_W_proj', 'L1_gnn_a_w', 'L1_gnn_bias']


def kernel(**inputs):
    import numpy as _np
    import concourse.bacc as _bacc
    from concourse import mybir as _mybir
    from concourse.bass_utils import run_bass_kernel_spmd as _run

    nc = _bacc.Bacc("TRN2", target_bir_lowering=False, num_devices=1)
    arrays, args = {}, []
    for name in _INS:
        a = _np.ascontiguousarray(inputs[name])
        arrays[f"in_{name}_dram"] = a
        args.append(nc.dram_tensor(f"in_{name}_dram", a.shape, _mybir.dt.from_np(a.dtype), kind="ExternalInput").ap())
    shape = tuple(inputs['x'].shape)
    args.append(nc.dram_tensor("out_0_dram", shape, _mybir.dt.float32, kind="ExternalOutput").ap())
    build_program(nc, *args)
    r = _run(nc, [arrays], core_ids=[0])
    return r.results[0]["out_0_dram"]
```

```python
import concourse.bass as bass
from concourse import mybir
from contextlib import ExitStack


def build_program(nc, x, adj, W, a, ln_g, ln_b, W1, b1, W2, b2, W3, b3, W_proj, a_w, bias, out):
    fp32 = mybir.dt.float32
    bf16 = mybir.dt.bfloat16
    ALU = mybir.AluOpType
    ACT = mybir.ActivationFunctionType
    AX_X = mybir.AxisListType.X

    B, N, D = x.shape
    P = 128
    DH = (a_w.shape[1] - 1) // 2
    H = D // DH
    K = 64
    GT = 4
    GROUP = GT * P
    NB = N // GROUP
    NG = B * NB
    JT = N // P
    HA = DH + 1
    HR = D + 2 * H
    CHUNK = 4
    NC_ = JT // CHUNK
    EPS = 1e-5
    PAD = 1.0000001111620804e-05
    BIG = 2.0 ** 100
    TINY = 1e-30
    LAG = 3
    HP = H - 1
    DIRECT = {7: 1, 12: 0, 13: 1, 15: 2}
    EARLY = (7,)
    LATE = (12, 13, 15)
    RELIEF = (12, 15)

    x1_d = nc.dram_tensor("x1_scratch", [NG, P, GT * D], fp32).ap()
    h_d = nc.dram_tensor("h_scratch", [NG, P, GT * HR], fp32).ap()
    rho_d = nc.dram_tensor("rho_scratch", [B, H * JT, P], fp32).ap()

    x_g = x.rearrange("b (g t p) f -> (b g) p t f", p=P, t=GT)
    out_g = out.rearrange("b (g t p) f -> (b g) p t f", p=P, t=GT)
    h_b = h_d.rearrange("(b g) p c -> b p g c", g=NB)
    rho_b = rho_d.rearrange("b (h g t) i -> b g h (t i)", h=H, g=NB)
    adj_g = adj.rearrange("b (g t p) j -> (b g) p t j", p=P, t=GT)

    ctx = ExitStack()
    with ctx:
        def sb(name, shape, dt=fp32):
            return ctx.enter_context(nc.sbuf_tensor(name, shape, dt))

        def sem(name):
            return ctx.enter_context(nc.semaphore(name))

        def bc(ap, axis, shape):
            return ap.unsqueeze(axis).broadcast_to(shape)

        ident = sb("ident", [P, P])
        ones = sb("ones", [H, P])
        ones_row = sb("ones_row", [1, GROUP])
        tiny = sb("tiny", [P, 1])
        zero = sb("zero", [P, GT])
        mhalf = sb("mhalf", [P, GT])
        eps_c = sb("eps_c", [P, GT])
        pen_bias = sb("pen_bias", [P, 1])
        neg_ident = sb("neg_ident", [P, P], bf16)
        sgn_ident = sb("sgn_ident", [P, P], bf16)
        we_raw = sb("we_raw", [P, 1])
        we_s = sb("we_s", [P, 8])
        W_sb = sb("W_sb", [P, D + 1])
        WT = sb("WT", [P, D])
        a_sb = sb("a_sb", [P, 1])
        W1_sb = sb("W1_sb", [P, D])
        W2_sb = sb("W2_sb", [P, D])
        W3_sb = sb("W3_sb", [P, D])
        b1_sb = sb("b1_sb", [P, 1])
        b2_sb = sb("b2_sb", [P, 1])
        b3_row = sb("b3_row", [1, D])
        g_bc = sb("g_bc", [P, D])
        b_bc = sb("b_bc", [P, D])
        bias_bc = sb("bias_bc", [P, D])
        Wp_sb = sb("Wp_sb", [P, D])
        WpT = sb("WpT", [P, HR])
        wlr = sb("wlr", [P, 2 * H])

        NX = 4
        X = [sb(f"X{r}", [P, H, GROUP]) for r in range(NX)]

        U = range(NB)
        assert NB == NX
        ST = [X[u][:, 0, :] for u in U]
        act_T = [X[u][:, 1, :] for u in U]
        yb = [X[u][:, 2, :] for u in U]
        zn = [yb[u].rearrange("p (t f) -> p t f", t=GT) for u in U]
        xg = [X[u][:, 3, :].rearrange("p (t f) -> p t f", t=GT) for u in U]
        blk = [sb(f"blk{u}", [P, GT, K]) for u in U]
        whe = [sb(f"whe{u}", [P, GT, D + 1]) for u in U]
        e_l = [sb(f"e_l{u}", [P, GT]) for u in U]
        ex = [sb(f"ex{u}", [P, GT, K]) for u in U]
        rmx = [sb(f"rmx{u}", [P, GT]) for u in U]
        rsm = [sb(f"rsm{u}", [P, GT]) for u in U]
        S = [sb(f"S{u}", [P, GT, P]) for u in U]
        st6 = [sb(f"st6{u}", [P, GT, 6]) for u in U]
        mv = [sb(f"mv{u}", [P, GT, 2]) for u in U]
        ve = [sb(f"ve{u}", [P, GT]) for u in U]
        rstd = [sb(f"rstd{u}", [P, GT]) for u in U]

        NG_ = 4
        NE = 4
        NPEN = 8
        LEAD = 4
        adj_sb = [sb(f"adj_sb{c}", [P, GT, CHUNK * P]) for c in range(NC_)]
        pen = [sb(f"pen{r}", [P, GT, P], bf16) for r in range(NPEN)]
        E = [sb(f"E{r}", [P, GROUP]) for r in range(NE)]
        G = [sb(f"G{r}", [P, GROUP]) for r in range(NG_)]
        RHO = sb("RHO", [P, 2, H, GROUP])
        hb = sb("hb", [P, JT, HR])
        lam = sb("lam", [P, JT, H])
        row_bias = sb("row_bias", [P, GT])
        B_nat = [sb(f"B_nat{r}", [P, GT, P]) for r in range(3)]
        rho_n = sb("rho_n", [P, H * JT])
        rho_T = sb("rho_T", [H * JT, P])
        rm = sb("rm", [P, H])
        R4 = sb("R4", [H, 1])
        diagR = sb("diagR", [H, H])
        Rb = sb("Rb", [P, H])
        sig = sb("sig", [P, JT, H])
        s_next = sb("s_next", [P, JT, H])
        s_j = sb("s_j", [P, JT, H])
        v_j = sb("v_j", [P, JT, H])
        haug = sb("haug", [P, JT, H, HA])
        hmean = sb("hmean", [1, H, HA])
        accU = sb("accU", [P, 2, GROUP])
        natO = sb("natO", [P, 2, GT, P])
        rden = sb("rden", [P, 2, GT, 2])
        x1b = sb("x1b", [P, GT, D])
        xbias = sb("xbias", [P, GT, D])
        res = sb("res", [P, GT, D])
        lky = sb("lky", [P, GT, D])
        est6 = sb("est6", [P, GT, 6])
        emv = sb("emv", [P, GT, 2])
        eve = sb("eve", [P, GT])
        erstd = sb("erstd", [P, GT])
        eprod = sb("eprod", [P, GT])
        eshift = sb("eshift", [P, GT])
        o_sb = sb("o_sb", [P, GT, D])

        x1T = [E[u][:] for u in U]
        xb = [G[u][:].rearrange("p (t f) -> p t f", t=GT) for u in U]
        h_o = [hb[:, u * GT:(u + 1) * GT, :] for u in U]
        assert NE == NG_ == NB

        psum = ctx.enter_context(nc.psum_tensor("psum", [P, 8, GROUP], fp32))
        bank = [psum[:, i, :] for i in range(8)]
        BA = bank[0:4]
        BB = bank[4:8]
        TA = bank[0:4]
        NT = len(TA)
        LB = bank[4:6]
        ACC = bank[6:8]

        const_set = sem("const_set")
        weights_in = sem("weights_in")
        prep_pe = sem("prep_pe")
        prep_dve = sem("prep_dve")
        prep_act = sem("prep_act")
        x_in = [sem(f"x_in{u}") for u in U]
        xT_ps = [sem(f"xT_ps{u}") for u in U]
        xT_sb = sem("xT_sb")
        wh_ps = sem("wh_ps")
        wh_sb = sem("wh_sb")
        xb_sb = [sem(f"xb_sb{u}") for u in U]
        scores_sb = [sem(f"scores_sb{u}") for u in U]
        exp_sb = sem("exp_sb")
        soft_sb = sem("soft_sb")
        ST_ps = sem("ST_ps")
        ST_sb = sem("ST_sb")
        oT_ps = sem("oT_ps")
        oT_sb = sem("oT_sb")
        y1_ps = sem("y1_ps")
        y1_b = sem("y1_b")
        y1_sb = sem("y1_sb")
        y2_ps = sem("y2_ps")
        y2_b = sem("y2_b")
        y2_sb = sem("y2_sb")
        z_ps = [sem(f"z_ps{u}") for u in U]
        var_z = sem("var_z")
        rstd_z = sem("rstd_z")
        zn_sb = [sem(f"zn_sb{u}") for u in U]
        r_sb = [sem(f"r_sb{u}") for u in U]
        var_r = sem("var_r")
        rstd_r = sem("rstd_r")
        x1_sb = [sem(f"x1_sb{u}") for u in U]
        x1T_ps = sem("x1T_ps")
        x1T_sb = sem("x1T_sb")
        h_ps = sem("h_ps")
        h_sb = [sem(f"h_sb{u}") for u in U]
        stored = [sem(f"stored{u}") for u in U]
        dve0 = sem("dve0")
        pool0 = sem("pool0")
        adj_in = [sem(f"adj_in{c}") for c in range(NC_)]
        pen_sb = sem("pen_sb")
        adjT_ps = sem("adjT_ps")
        G_sb = sem("G_sb")
        E_sb = sem("E_sb")
        B_pool = sem("B_pool")
        B_dve = sem("B_dve")
        X_sb = sem("X_sb")
        pv_done = sem("pv_done")
        rho_st = sem("rho_st")
        rho_in = sem("rho_in")
        s_sb = sem("s_sb")
        shift_sb = sem("shift_sb")
        accU_sb = sem("accU_sb")
        nat_ps = sem("nat_ps")
        nat_sb = sem("nat_sb")
        hb_in = sem("hb_in")
        rm_sb = sem("rm_sb")
        rmT_ps = sem("rmT_ps")
        diag_sb = sem("diag_sb")
        Rb_ps = sem("Rb_ps")
        sig_sb = sem("sig_sb")
        sv_sb = sem("sv_sb")
        lam_sb = sem("lam_sb")
        rho_n_sb = sem("rho_n_sb")
        rho_ps = sem("rho_ps")
        rho_sb = sem("rho_sb")
        hv_sb = sem("hv_sb")
        haug_sb = sem("haug_sb")
        hsum_ps = sem("hsum_ps")
        hmean_sb = sem("hmean_sb")
        res_sb = sem("res_sb")
        x1_in = sem("x1_in")
        xbias_sb = sem("xbias_sb")
        evar = sem("evar")
        o_done = sem("o_done")
        out_st = sem("out_st")
        dve_b = sem("dve_b")
        dve_e = sem("dve_e")
        row_bias_sb = sem("row_bias_sb")
        BT_early = sem("BT_early")
        BT_late = sem("BT_late")
        pool_turn = sem("pool_turn")
        pool_e = sem("pool_e")

        N_WEIGHTS = 13 + 2 * H
        N_CONST = 15
        POOL0, DVE0, DVE_B, DVE_E, POOL_E = 12, 20, 3, 4, 3

        def chain(eng, semaphore, base):
            count = [0]

            def link(ins):
                count[0] += 1
                ins.then_inc(semaphore, 1)
                eng.wait_ge(semaphore, base + count[0])
            return link, count

        HEAD = 8

        def walk(eng, prepare, tile, epilogue):
            def step(b, g, ib, crossing):
                for k in range(HEAD, JT):
                    if crossing:
                        prepare(b + 1, k)
                    tile(b, g, ib, k, crossing)
                for k in range(HEAD):
                    tile(b + 1 if crossing else b, g + 1, 0 if crossing else ib + 1, k, crossing)
                    epilogue(g, k)

            for k in range(HEAD, JT):
                prepare(0, k)
            for k in range(HEAD):
                tile(0, 0, 0, k, True)
            with eng.Fori(0, B - 1) as b:
                with eng.Fori(0, NB - 1) as ib:
                    step(b, b * NB + ib, ib, False)
                step(b, b * NB + (NB - 1), NB - 1, True)
            with eng.Fori(0, NB - 1) as ib:
                step(B - 1, ib + (B - 1) * NB, ib, False)
            for k in range(HEAD, JT):
                tile(B - 1, NG - 1, NB - 1, k, False)
            for k in range(HEAD):
                epilogue(NG - 1, k)

        def walk0(eng, first, middle, last, head=lambda: None):
            first(0)
            head()
            with eng.Fori(0, B - 1) as b:
                middle(b)
                first(b + 1)
                last(b)
            middle(B - 1)
            last(B - 1)

        def direct(k, crossing):
            return k in EARLY or (k in LATE and not crossing)

        def is_last(g):
            return isinstance(g, int) and g == NG - 1

        block = ctx.enter_context(nc.Block())

        @block.sync
        def _(sp):
            for dst, src in ((W_sb[:, 0:D], W), (a_sb[:], a), (W1_sb[:], W1), (W2_sb[:], W2), (W3_sb[:], W3),
                             (b1_sb[:], b1.unsqueeze(1)), (b2_sb[:], b2.unsqueeze(1)), (b3_row[:], b3.unsqueeze(0)),
                             (g_bc[:], ln_g.partition_broadcast(P)), (b_bc[:], ln_b.partition_broadcast(P)),
                             (bias_bc[:], bias.partition_broadcast(P)), (Wp_sb[:], W_proj),
                             (we_raw[:], a_w[0, 2 * DH:2 * DH + 1].partition_broadcast(P))):
                sp.dma_start(dst, src).then_inc(weights_in, 16)
            sp.wait_ge(const_set, 1)
            for h in range(H):
                for side in range(2):
                    sp.dma_start(wlr[h * DH:(h + 1) * DH, (1 - side) * H + h:(1 - side) * H + h + 1],
                                 a_w[0, side * DH:(side + 1) * DH].unsqueeze(1)).then_inc(weights_in, 16)

            sp.sem_inc(res_sb, 1)
            sp.sem_inc(out_st, 1)
            for u in U:
                sp.sem_inc(xb_sb[u], 1)
                sp.sem_inc(xT_ps[u], 1)
                sp.sem_inc(scores_sb[u], 1)
                for free in (h_sb, stored, zn_sb, z_ps, r_sb):
                    sp.sem_inc(free[u], 1)

            with sp.Fori(0, B) as b:
                for u in U:
                    sp.wait_ge(xb_sb[u], b + 1)
                    sp.wait_ge(xT_ps[u], b + 1)
                    sp.wait_ge(scores_sb[u], b + 1)
                    sp.dma_start(xg[u], x_g[b * NB + u]).then_inc(x_in[u], 16)
                    for q in range(2):
                        at = b * (N * N) + (u * GROUP + q * K) * (N + 1)
                        sp.dma_start(blk[u][q * K:(q + 1) * K],
                                     bass.AP(adj.tensor, at, [[N, K], [P * (N + 1), GT], [1, K]])) \
                            .then_inc(x_in[u], 16)

            def load_adj(g, c):
                sp.dma_start(adj_sb[c][:], adj_g[g][:, :, c * CHUNK * P:(c + 1) * CHUNK * P]).then_inc(adj_in[c], 16)

            LOAD_AT = (HEAD, HEAD + 1, HEAD + 4, HEAD + 6)

            def load_batch(b):
                sp.dma_start(hb[:].rearrange("p (g t) c -> p g (t c)", g=NB), h_b[b]).then_inc(hb_in, 16)

            for c in range(NC_):
                load_adj(0, c)
            for u in U:
                sp.wait_ge(stored[u], 2 * 16 * B + 1)
            sp.dma_start(x1b[:], x1_d[0]).then_inc(x1_in, 16)

            def load_rho(b, ib):
                sp.dma_start(RHO[:, ib % 2], rho_b[b][ib].partition_broadcast(P)).then_inc(rho_in, 16)

            def prepare(b, k):
                if k == HEAD:
                    if not (isinstance(b, int) and b == 0):
                        sp.wait_ge(haug_sb, 2 * NC_ * b)
                        sp.wait_ge(hsum_ps, b)
                        sp.wait_ge(lam_sb, b)
                    load_batch(b)
                if k == JT - 2:
                    sp.wait_ge(rho_sb, b + 1)
                    sp.dma_start(rho_d[b], rho_T[:]).then_inc(rho_st, 16)
                    sp.wait_ge(rho_st, 16 * (b + 1))
                    load_rho(b, 0)

            def tile(b, g, ib, k, crossing):
                if k in LOAD_AT and not is_last(g):
                    c = LOAD_AT.index(k)
                    sp.wait_ge(adjT_ps, JT * g + CHUNK * (c + 1))
                    load_adj(g + 1, c)
                if k == HEAD + 2 and not crossing and not is_last(g):
                    if not (isinstance(g, int) and g == 0):
                        sp.wait_ge(X_sb, JT * g + 1)
                    load_rho(b, ib + 1)

            def epilogue(g, k):
                if k == HEAD - 1:
                    sp.wait_ge(o_done, GT * (g + 1))
                    sp.dma_start(out_g[g], o_sb[:]).then_inc(out_st, 16)
                    if not is_last(g):
                        sp.dma_start(x1b[:], x1_d[g + 1]).then_inc(x1_in, 16)

            walk(sp, prepare, tile, epilogue)
            sp.wait_ge(out_st, 16 * NG + 1)

        @block.gpsimd
        def _(pool):
            nc.gpsimd.memset(wlr[:], 0.0).then_inc(const_set, 1)
            nc.gpsimd.memset(ident[:], 0.0).then_inc(const_set, 1)
            nc.gpsimd.memset(ones[:], 1.0).then_inc(const_set, 1)
            nc.gpsimd.memset(ones_row[:], 1.0).then_inc(const_set, 1)
            nc.gpsimd.memset(tiny[:], TINY).then_inc(const_set, 1)
            nc.gpsimd.memset(mhalf[:], -0.5).then_inc(const_set, 1)
            nc.gpsimd.memset(zero[:], 0.0).then_inc(const_set, 1)
            nc.gpsimd.memset(eps_c[:], EPS).then_inc(const_set, 1)
            nc.gpsimd.memset(hmean[:], N * TINY).then_inc(const_set, 1)
            nc.gpsimd.memset(accU[:], 0.0).then_inc(const_set, 1)
            for u in U:
                nc.gpsimd.memset(S[u][:], 0.0).then_inc(const_set, 1)
            pool.wait_ge(const_set, N_CONST - 1)
            nc.gpsimd.affine_select(out=ident[:], in_=ident[:], compare_op=ALU.not_equal, fill=1.0, base=0,
                                    pattern=[[-1, P]], channel_multiplier=1).then_inc(const_set, 1)

            pool.wait_ge(weights_in, 16 * N_WEIGHTS)
            with pool.Fori(0, B) as b:
                link, steps = chain(pool, pool0, b * POOL0)
                for u in U:
                    pool.wait_ge(x_in[u], 3 * 16 * (b + 1))
                    pool.wait_ge(r_sb[u], b + 1)
                    nc.gpsimd.tensor_tensor(xb[u], xg[u], bc(b_bc[:], 1, [P, GT, D]), ALU.add).then_inc(xb_sb[u], 1)

                def z_rstd(u):
                    pool.wait_ge(var_z, GT * (NB * b + u + 1))
                    link(nc.gpsimd.tensor_tensor(ve[u][:], mv[u][:, :, 1], eps_c[:], ALU.add))
                    nc.gpsimd.tensor_tensor(rstd[u][:], ve[u][:], mhalf[:], ALU.pow).then_inc(rstd_z, 1)

                def residual(u):
                    pool.wait_ge(zn_sb[u], GT * (b + 1) + 1)
                    link(nc.gpsimd.tensor_tensor(zn[u], zn[u], bc(g_bc[:], 1, [P, GT, D]), ALU.mult))
                    nc.gpsimd.tensor_tensor(zn[u], zn[u], xb[u], ALU.add).then_inc(r_sb[u], 1)

                def r_rstd(u):
                    pool.wait_ge(var_r, GT * (NB * b + u + 1))
                    link(nc.gpsimd.tensor_tensor(ve[u][:], mv[u][:, :, 1], eps_c[:], ALU.add))
                    nc.gpsimd.tensor_tensor(rstd[u][:], ve[u][:], mhalf[:], ALU.pow).then_inc(rstd_r, 1)

                z_rstd(0)
                z_rstd(1)
                residual(0)
                z_rstd(2)
                residual(1)
                z_rstd(3)
                r_rstd(0)
                residual(2)
                r_rstd(1)
                residual(3)
                r_rstd(2)
                r_rstd(3)
                assert steps[0] == POOL0

            def prepare(b, k):
                pass

            def tile(b, g, ib, k, crossing):
                m = JT * g + k
                if k == 0:
                    pool.wait_ge(rho_in, 16 * (g + 1))
                if not (isinstance(g, int) and g == 0 and k < NX):
                    pool.wait_ge(pv_done, m - NX + 1)
                pool.wait_ge(E_sb, m + 1)
                pool.sem_inc(pool_turn, 1)
                heads = HP - 1 if direct(k, crossing) and k in RELIEF else HP
                nc.gpsimd.tensor_tensor(X[k % NX][:, 0:heads, :], RHO[:, ib % 2, 0:heads, :],
                                        bc(E[k % NE][:], 1, [P, heads, GROUP]), ALU.mult).then_inc(B_pool, 1)

            def epilogue(g, k):
                link, steps = chain(pool, pool_e, g * POOL_E)
                if k == 2:
                    pool.wait_ge(x1_in, 16 * (g + 1))
                    nc.gpsimd.tensor_tensor(xbias[:], x1b[:], bc(bias_bc[:], 1, [P, GT, D]),
                                            ALU.add).then_inc(xbias_sb, 1)
                if k == 5:
                    pool.wait_ge(evar, GT * (g + 1))
                    link(nc.gpsimd.tensor_tensor(eve[:], emv[:, :, 1], eps_c[:], ALU.add))
                    link(nc.gpsimd.tensor_tensor(erstd[:], eve[:], mhalf[:], ALU.pow))
                    link(nc.gpsimd.tensor_tensor(eprod[:], emv[:, :, 0], erstd[:], ALU.mult))
                    nc.gpsimd.tensor_tensor(eshift[:], zero[:], eprod[:], ALU.subtract).then_inc(shift_sb, 1)

            walk(pool, prepare, tile, epilogue)

        @block.scalar
        def _(act):
            def copy(dst, src):
                return nc.scalar.activation(dst, src, ACT.Copy)

            act.wait_ge(prep_pe, 1)
            copy(WT[:], bank[0][:, 0:D]).then_inc(prep_act, 1)
            act.wait_ge(prep_pe, 2)
            copy(WpT[:, 0:D], bank[1][:, 0:D]).then_inc(prep_act, 1)
            act.wait_ge(prep_pe, 3)
            copy(WpT[:, D:HR], bank[2][:, 0:2 * H]).then_inc(prep_act, 1)
            act.wait_ge(prep_pe, 4)
            copy(W_sb[:, D:D + 1], bank[3][:, 0:1]).then_inc(prep_act, 1)

            def first(b):
                for u in U:
                    act.wait_ge(xT_ps[u], b + 2)
                    act.wait_ge(z_ps[u], b + 1)
                    copy(act_T[u], BA[u]).then_inc(xT_sb, 1)
                for u in U:
                    act.wait_ge(wh_ps, NB * b + u + 1)
                    for half, bk in ((1, BA), (0, BB)):
                        copy(whe[u][:, 2 * half:2 * half + 2, :],
                             bk[u][:, 0:2 * (D + 1)].rearrange("p (t c) -> p t c", t=2)).then_inc(wh_sb, 1)

            def exp_blocks(b, u):
                act.wait_ge(scores_sb[u], b + 2)
                nc.scalar.activation(ex[u][:], ex[u][:], ACT.Exp).then_inc(exp_sb, 1)

            def middle(b):
                n = [NB * b + u + 1 for u in U]
                for u in U:
                    act.wait_ge(ST_ps, n[u])
                    copy(ST[u], BB[u]).then_inc(ST_sb, 1)
                for u in U:
                    act.wait_ge(oT_ps, n[u])
                    copy(act_T[u], BA[u]).then_inc(oT_sb, 1)
                for u in U:
                    act.wait_ge(y1_ps, n[u])
                    act.wait_ge(stored[u], 2 * 16 * b + 1)
                    nc.scalar.activation(yb[u], BB[u], ACT.Identity, bias=b1_sb[:]).then_inc(y1_b, 1)
                for u in U:
                    act.wait_ge(y2_ps, n[u])
                    nc.scalar.activation(yb[u], BA[u], ACT.Identity, bias=b2_sb[:]).then_inc(y2_b, 1)

            def last(b):
                n = [NB * b + u + 1 for u in U]
                for u in U:
                    act.wait_ge(x1_sb[u], GT * (b + 1))
                    act.dma_start(x1_d[NB * b + u], yb[u]).then_inc(stored[u], 16)
                    act.wait_ge(x1T_ps, n[u])
                    copy(x1T[u], BA[u]).then_inc(x1T_sb, 1)
                for u in U:
                    if not isinstance(b, int):
                        exp_blocks(b + 1, u)
                    act.wait_ge(h_ps, n[u])
                    for half, bk in ((0, BB), (1, BA)):
                        copy(h_o[u][:, 2 * half:2 * half + 2, :],
                             bk[u][:, 0:2 * HR].rearrange("p (t c) -> p t c", t=2)).then_inc(h_sb[u], 1)
                for u in U:
                    act.wait_ge(h_sb[u], 2 * b + 3)
                    act.dma_start(h_d[NB * b + u], h_o[u].rearrange("p t c -> p (t c)")).then_inc(stored[u], 16)

            def head():
                for u in U:
                    exp_blocks(0, u)

            walk0(act, first, middle, last, head)

            act.wait_ge(prep_dve, 11)

            def penalty(g, k):
                c = k // CHUNK
                act.wait_ge(adj_in[c], 16 * (g + 1))
                if not (isinstance(g, int) and g == 0 and k < NPEN):
                    act.wait_ge(adjT_ps, JT * g + k - NPEN + 1)
                nc.scalar.activation(pen[k % NPEN][:], adj_sb[c][:, :, (k % CHUNK) * P:(k % CHUNK + 1) * P],
                                     ACT.Relu, scale=-BIG, bias=pen_bias[:]).then_inc(pen_sb, 1)

            def rows_last_head(g, k):
                act.wait_ge(adj_in[k // CHUNK], 16 * (g + 1))
                for t in range(GT):
                    nc.scalar.activation(B_nat[DIRECT[k]][:, t, :],
                                         adj_sb[k // CHUNK][:, t, (k % CHUNK) * P:(k % CHUNK + 1) * P],
                                         ACT.Exp, scale=we_s[:, 3:4], bias=row_bias[:, t:t + 1])

            for k in range(LEAD):
                penalty(0, k)

            def prepare(b, k):
                if k == HEAD + 5:
                    act.wait_ge(lam_sb, b + 1)
                    nc.scalar.activation(rho_n[:].rearrange("p (h t) -> p h t", h=H), lam[:].rearrange("p t h -> p h t"),
                                         ACT.Exp, scale=-0.8).then_inc(rho_n_sb, 1)
                    if not (isinstance(b, int) and b == 0):
                        act.wait_ge(s_sb, b)
                        act.wait_ge(haug_sb, 2 * NC_ * b)
                    act.wait_ge(sig_sb, b + 1)
                    nc.scalar.activation(s_next[:], sig[:], ACT.Exp, scale=0.8).then_inc(sv_sb, 1)
                    nc.scalar.activation(v_j[:], sig[:], ACT.Exp, scale=0.2).then_inc(sv_sb, 1)
                if k == HEAD + 6:
                    act.wait_ge(rho_ps, b + 1)
                    if not (isinstance(b, int) and b == 0):
                        act.wait_ge(rho_st, 16 * b)
                    copy(rho_T[:], LB[0][0:H * JT, 0:P]).then_inc(rho_sb, 1)
                if k == HEAD + 7:
                    act.wait_ge(hsum_ps, b + 1)
                    nc.scalar.activation(hmean[:, :, 0:DH], LB[1][0:1, 0:D].rearrange("p (h d) -> p h d", h=H),
                                         ACT.Copy).then_inc(hmean_sb, 1)

            def tile(b, g, ib, k, crossing):
                m = JT * g + k
                if crossing and 3 <= k < 3 + NC_:
                    if k == 3:
                        act.wait_ge(hv_sb, b + 1)
                    q = slice((k - 3) * CHUNK, (k - 2) * CHUNK)
                    copy(haug[:, q, :, 0:DH], hb[:, q, 0:D].rearrange("p t (h d) -> p t h d", h=H)).then_inc(haug_sb, 1)
                    copy(haug[:, q, :, DH], v_j[:, q]).then_inc(haug_sb, 1)
                act.wait_ge(adjT_ps, m + 1)
                if not (isinstance(g, int) and g == 0 and k < NE):
                    act.wait_ge(X_sb, m - NE + 1)
                nc.scalar.activation(E[k % NE][:], TA[k % NT], ACT.Exp, scale=we_s[:, 3:4],
                                     bias=we_s[:, 5:6]).then_inc(E_sb, 1)
                nc.scalar.activation(G[k % NG_][:], TA[k % NT], ACT.Exp, scale=we_s[:, 2:3],
                                     bias=we_s[:, 4:5]).then_inc(G_sb, 1)
                if k == 1:
                    nc.scalar.activation(row_bias[:], lam[:, bass.ts(ib, GT), HP], ACT.Identity, scale=-0.8,
                                         bias=we_s[:, 5:6]).then_inc(row_bias_sb, 1)
                if direct(k + LEAD, crossing):
                    if k + LEAD == EARLY[0]:
                        act.wait_ge(row_bias_sb, g + 1)
                    rows_last_head(g, k + LEAD)
                if k + LEAD < JT:
                    penalty(g, k + LEAD)
                elif not is_last(g):
                    penalty(g + 1, k + LEAD - JT)

            def epilogue(g, k):
                if k == 2:
                    act.wait_ge(pv_done, JT * (g + 1))
                    for a_ in range(2):
                        rows = slice(64 * a_, 64 * a_ + HA)
                        copy(accU[rows], psum[rows, 6:8, :]).then_inc(accU_sb, 1)
                if k == 4:
                    act.wait_ge(res_sb, 2 * g + 1)
                    for r in range(2):
                        act.wait_ge(nat_ps, 2 * g + r + 1)
                        copy(natO[:, r].rearrange("p t f -> p (t f)"), LB[r]).then_inc(nat_sb, 1)
                if k == 7:
                    act.wait_ge(shift_sb, g + 1)
                    act.wait_ge(out_st, 16 * g + 1)
                    for t in range(GT):
                        nc.scalar.activation(o_sb[:, t, :], lky[:, t, :], ACT.Identity, scale=erstd[:, t:t + 1],
                                             bias=eshift[:, t:t + 1]).then_inc(o_done, 1)

            walk(act, prepare, tile, epilogue)

        @block.vector
        def _(dve):
            V = nc.vector
            dve.wait_ge(weights_in, 16 * N_WEIGHTS)
            dve.wait_ge(const_set, N_CONST)
            link, _ = chain(dve, prep_dve, 0)
            w = [we_s[:, i:i + 1] for i in range(8)]
            link(V.tensor_scalar(w[0], we_raw[:], 0.0, 2.0, ALU.is_ge, ALU.mult))
            link(V.tensor_scalar(w[0], w[0], -1.0, None, ALU.add))
            link(V.tensor_scalar(w[1], we_raw[:], w[0], 1e-10, ALU.mult, ALU.max))
            link(V.tensor_scalar(w[2], w[1], w[0], None, ALU.mult))
            link(V.tensor_scalar(w[7], w[2], 0.0, None, ALU.max))
            link(V.tensor_scalar(w[3], w[2], 0.2, None, ALU.mult))
            link(V.tensor_scalar(w[4], w[7], -1.0, None, ALU.mult))
            link(V.tensor_scalar(w[5], w[7], -0.2, None, ALU.mult))
            link(V.tensor_scalar(sgn_ident[:], ident[:], w[0], -1.0, ALU.mult, ALU.mult))
            link(V.tensor_scalar(neg_ident[:], ident[:], -1.0, None, ALU.mult))
            link(V.memset(pen_bias[:], BIG * PAD))

            def normalise(link, src, stats, mean_var, done):
                for t in range(GT):
                    V.bn_stats(stats[:, t, :], src(t))
                dve.drain()
                for t in range(GT):
                    V.bn_aggr(mean_var[:, t, :], stats[:, t, :]).then_inc(done, 1)

            with dve.Fori(0, B) as b:
                link, steps = chain(dve, dve0, b * DVE0)
                n = [NB * b + u + 1 for u in U]
                for u in U:
                    dve.wait_ge(wh_sb, 2 * n[u])
                    wa = whe[u][:, :, D]
                    link(V.scalar_tensor_tensor(e_l[u][:], wa, 0.2, wa, ALU.mult, ALU.max))
                    dve.wait_ge(x_in[u], 3 * 16 * (b + 1))
                    link(V.tensor_tensor(ex[u][:], blk[u][:], bc(e_l[u][:], 2, [P, GT, K]), ALU.mult))
                    link(V.reduce_max(rmx[u][:], ex[u][:], AX_X))
                    V.tensor_tensor(ex[u][:], ex[u][:], bc(rmx[u][:], 2, [P, GT, K]),
                                    ALU.subtract).then_inc(scores_sb[u], 1)
                for u in U:
                    dve.wait_ge(exp_sb, n[u])
                    link(V.reduce_sum(rsm[u][:], ex[u][:], AX_X))
                    link(V.reciprocal(rsm[u][:], rsm[u][:]))
                    for q in range(2):
                        rows = slice(q * K, (q + 1) * K)
                        V.tensor_tensor(S[u][rows, :, rows], ex[u][rows],
                                        bc(rsm[u][rows], 2, [K, GT, K]), ALU.mult).then_inc(soft_sb, 1)
                for u in U:
                    dve.wait_ge(y1_b, n[u])
                    V.scalar_tensor_tensor(act_T[u], yb[u], 0.01, yb[u], ALU.mult, ALU.max).then_inc(y1_sb, 1)
                for u in U:
                    dve.wait_ge(y2_b, n[u])
                    V.scalar_tensor_tensor(act_T[u], yb[u], 0.01, yb[u], ALU.mult, ALU.max).then_inc(y2_sb, 1)
                def z_stats(u):
                    dve.wait_ge(z_ps[u], b + 2)
                    normalise(link, lambda t: BB[u][:, t * D:(t + 1) * D], st6[u], mv[u], var_z)

                def z_norm(u):
                    dve.wait_ge(rstd_z, n[u])
                    for t in range(GT):
                        V.tensor_scalar(zn[u][:, t, :], BB[u][:, t * D:(t + 1) * D], mv[u][:, t, 0:1],
                                        rstd[u][:, t:t + 1], ALU.subtract, ALU.mult).then_inc(zn_sb[u], 1)

                def r_stats(u):
                    dve.wait_ge(r_sb[u], b + 2)
                    normalise(link, lambda t: zn[u][:, t, :], st6[u], mv[u], var_r)

                def r_norm(u):
                    dve.wait_ge(rstd_r, n[u])
                    for t in range(GT):
                        V.tensor_scalar(zn[u][:, t, :], zn[u][:, t, :], mv[u][:, t, 0:1],
                                        rstd[u][:, t:t + 1], ALU.subtract, ALU.mult).then_inc(x1_sb[u], 1)

                z_stats(0)
                z_stats(1)
                z_norm(0)
                z_stats(2)
                z_norm(1)
                z_stats(3)
                r_stats(0)
                z_norm(2)
                r_stats(1)
                r_norm(0)
                z_norm(3)
                r_stats(2)
                r_norm(1)
                r_stats(3)
                r_norm(2)
                r_norm(3)
                assert steps[0] == DVE0, steps

            def prepare(b, k):
                link, steps = chain(dve, dve_b, b * DVE_B)
                if k == HEAD + 1:
                    dve.wait_ge(hb_in, 16 * (b + 1))
                    V.reduce_max(rm[:], hb[:, :, D:D + H].rearrange("p t h -> p h t"), AX_X).then_inc(rm_sb, 1)
                if k == HEAD + 2:
                    dve.wait_ge(rmT_ps, b + 1)
                    link(V.reduce_max(R4[:], LB[0][0:H, 0:P], AX_X))
                    V.tensor_scalar(diagR[:], ident[0:H, 0:H], R4[:], None, ALU.mult).then_inc(diag_sb, 1)
                if k == HEAD + 3:
                    steps[0] = 1
                    dve.wait_ge(Rb_ps, b + 1)
                    link(V.tensor_copy(Rb[:], LB[0][:, 0:H]))
                    if not (isinstance(b, int) and b == 0):
                        dve.wait_ge(row_bias_sb, NB * b)
                    link(V.tensor_tensor(lam[:], hb[:, :, D + H:HR], bc(Rb[:], 1, [P, JT, H]), ALU.add))
                    V.tensor_scalar(lam[:], lam[:], we_s[:, 7:8], -50.0, ALU.add, ALU.max).then_inc(lam_sb, 1)
                    V.tensor_tensor(sig[:], hb[:, :, D:D + H], bc(Rb[:], 1, [P, JT, H]),
                                    ALU.subtract).then_inc(sig_sb, 1)
                if k == HEAD + 6:
                    dve.wait_ge(hsum_ps, b + 1)
                    dve.wait_ge(sv_sb, 2 * (b + 1))
                    h_rows = hb[:, :, 0:D].rearrange("p t (h d) -> p t h d", h=H)
                    V.tensor_tensor(h_rows, h_rows, bc(v_j[:], 3, [P, JT, H, DH]), ALU.mult).then_inc(hv_sb, 1)

            def tile(b, g, ib, k, crossing):
                m = JT * g + k
                slot = X[k % NX]
                if k == 0:
                    dve.wait_ge(rho_in, 16 * (g + 1))
                    if crossing:
                        dve.wait_ge(sv_sb, 2 * (b + 1))
                        if not (isinstance(g, int) and g == 0):
                            dve.wait_ge(X_sb, m)
                        V.tensor_copy(s_j[:], s_next[:]).then_inc(s_sb, 1)
                        dve.wait_ge(s_sb, b + 1)
                if not (isinstance(g, int) and g == 0 and k < NX):
                    dve.wait_ge(pv_done, m - NX + 1)
                dve.wait_ge(E_sb, m + 1)
                is_direct = direct(k, crossing)
                own = HP if not is_direct else HP - 1 if k in RELIEF else None
                if own is not None:
                    V.tensor_tensor(slot[:, own, :], RHO[:, ib % 2, own, :], E[k % NE][:], ALU.mult).then_inc(B_dve, 1)
                dve.wait_ge(G_sb, m + 1)
                dve.wait_ge(B_pool, m + 1)
                if is_direct and k in EARLY:
                    dve.wait_ge(BT_early, len(EARLY) * g + EARLY.index(k) + 1)
                elif is_direct:
                    dve.wait_ge(BT_late, len(LATE) * (b * (NB - 1) + ib) + LATE.index(k) + 1)
                for h in range(H):
                    if h == own:
                        dve.wait_ge(B_dve, m + 1)
                    rho_E = LB[DIRECT[k] % 2] if h == HP and is_direct else slot[:, h, :]
                    ins = V.scalar_tensor_tensor(slot[:, h, :], G[k % NG_][:], s_j[:, k, h:h + 1], rho_E,
                                                 ALU.mult, ALU.max)
                    if h == 0 and own is None:
                        ins.then_inc(B_dve, 1)
                ins.then_inc(X_sb, 1)

            def epilogue(g, k):
                if k == 3:
                    link, steps = chain(dve, dve_e, g * DVE_E)
                    dve.wait_ge(nat_sb, 2 * (g + 1))
                    parts = natO[:].rearrange("p r t (a d) -> p r t a d", a=2)
                    link(V.reciprocal(rden[:], parts[:, :, :, :, DH]))
                    heads = res[:].rearrange("p t (r a d) -> p r t a d", r=2, a=2)
                    for r in range(2):
                        V.tensor_tensor(heads[:, r], parts[:, r, :, :, 0:DH], bc(rden[:, r], 3, [P, GT, 2, DH]),
                                        ALU.mult).then_inc(res_sb, 1)
                    dve.wait_ge(res_sb, 2 * (g + 1) + 1)
                    dve.wait_ge(xbias_sb, g + 1)
                    link(V.tensor_tensor(res[:], res[:], xbias[:], ALU.add))
                    link(V.scalar_tensor_tensor(lky[:], res[:], 0.5, res[:], ALU.mult, ALU.max))
                    link(V.tensor_tensor(lky[:], lky[:], x1b[:], ALU.add))
                    normalise(link, lambda t: lky[:, t, :], est6, emv, evar)
                    assert steps[0] == DVE_E, steps

            walk(dve, prepare, tile, epilogue)

        @block.tensor
        def _(pe):
            T = nc.tensor

            def mm(o, l, r, start=True, stop=True):
                return T.matmul(o, l, r, start=start, stop=stop)

            pe.wait_ge(weights_in, 16 * N_WEIGHTS)
            pe.wait_ge(const_set, N_CONST)
            T.transpose(bank[0][:, 0:D], W_sb[:, 0:D], ident[:]).then_inc(prep_pe, 1)
            T.transpose(bank[1][:, 0:D], Wp_sb[:], ident[:]).then_inc(prep_pe, 1)
            mm(bank[2][:, 0:2 * H], Wp_sb[:], wlr[:]).then_inc(prep_pe, 1)
            pe.wait_ge(prep_act, 1)
            mm(bank[3][:, 0:1], WT[:], a_sb[:]).then_inc(prep_pe, 1)
            pe.wait_ge(prep_act, 4)

            def tsl(t):
                return slice(t * P, (t + 1) * P)

            def first(b):
                for u in U:
                    pe.wait_ge(x_in[u], 3 * 16 * (b + 1))
                    for t in range(GT):
                        ins = T.transpose(BA[u][:, tsl(t)], xg[u][:, t, :], ident[:])
                    ins.then_inc(xT_ps[u], 1)
                for u in U:
                    pe.wait_ge(xT_sb, NB * b + u + 1)
                    for t in (2, 3, 0, 1):
                        if t == 0:
                            pe.wait_ge(zn_sb[u], GT * b + 1)
                        at = (t % 2) * (D + 1)
                        ins = mm((BB, BA)[t // 2][u][:, at:at + D + 1], act_T[u][:, tsl(t)], W_sb[:])
                    ins.then_inc(wh_ps, 1)

            def middle(b):
                n = [NB * b + u + 1 for u in U]
                for u in U:
                    pe.wait_ge(soft_sb, 2 * n[u])
                    pe.wait_ge(h_sb[u], 2 * b + 1)
                    for t in range(GT):
                        ins = T.transpose(BB[u][:, tsl(t)], S[u][:, t, :], ident[:])
                    ins.then_inc(ST_ps, 1)
                for u in U:
                    pe.wait_ge(ST_sb, n[u])
                    for t in range(GT):
                        ins = mm(BA[u][:, tsl(t)], whe[u][:, t, 0:D], ST[u][:, tsl(t)])
                    ins.then_inc(oT_ps, 1)
                for u in U:
                    pe.wait_ge(oT_sb, n[u])
                    mm(BB[u], W1_sb[:], act_T[u]).then_inc(y1_ps, 1)
                for u in U:
                    pe.wait_ge(y1_sb, n[u])
                    mm(BA[u], W2_sb[:], act_T[u]).then_inc(y2_ps, 1)
                for u in U:
                    pe.wait_ge(y2_sb, n[u])
                    for t in range(GT):
                        z = BB[u][:, tsl(t)]
                        mm(z, act_T[u][:, tsl(t)], W3_sb[:], stop=False)
                        mm(z, ST[u][:, tsl(t)], whe[u][:, t, 0:D], start=False, stop=False)
                        ins = mm(z, ones_row[0:1, 0:P], b3_row[:], start=False)
                    ins.then_inc(z_ps[u], 1)

            def last(b):
                n = [NB * b + u + 1 for u in U]
                for u in U:
                    pe.wait_ge(x1_sb[u], GT * (b + 1))
                    if isinstance(b, int):
                        pe.wait_ge(wh_sb, 2 * NB * B)
                    else:
                        pe.wait_ge(wh_sb, 2 * (NB * (b + 1) + u + 1))
                    for t in range(GT):
                        ins = T.transpose(BA[u][:, tsl(t)], zn[u][:, t, :], ident[:])
                    ins.then_inc(x1T_ps, 1)
                for u in U:
                    pe.wait_ge(x1T_sb, n[u])
                    for t in range(GT):
                        at = (t % 2) * HR
                        ins = mm((BB, BA)[t // 2][u][:, at:at + HR], x1T[u][:, tsl(t)], WpT[:])
                    ins.then_inc(h_ps, 1)

            walk0(pe, first, middle, last)

            for u in U:
                pe.wait_ge(h_sb[u], 2 * B + 1)
            pe.wait_ge(prep_dve, 11)

            def transpose_adj(g, k):
                m = JT * g + k
                c = k // CHUNK
                pe.wait_ge(pen_sb, m + 1)
                if not (isinstance(g, int) and g == 0 and k < NT):
                    pe.wait_ge(G_sb, m - NT + 1)
                for t in range(GT):
                    o = TA[k % NT][:, tsl(t)]
                    a0 = (k % CHUNK) * P
                    T.matmul(o, adj_sb[c][:, t, a0:a0 + P], ident[:], is_transpose=True, start=True, stop=False)
                    ins = mm(o, pen[k % NPEN][:, t, :], sgn_ident[:], start=False)
                ins.then_inc(adjT_ps, 1)

            def transpose_last_head(g, k, counter):
                for t in range(GT):
                    o = LB[DIRECT[k] % 2][:, tsl(t)]
                    T.matmul(o, B_nat[DIRECT[k]][:, t, :], ident[:], is_transpose=True, start=True, stop=False)
                    ins = mm(o, pen[k % NPEN][:, t, :], neg_ident[:], start=False)
                ins.then_inc(counter, 1)

            for k in range(LAG):
                transpose_adj(0, k)

            def prepare(b, k):
                if k == HEAD + 1:
                    pe.wait_ge(rm_sb, b + 1)
                    T.transpose(LB[0][0:H, 0:P], rm[:], ident[:]).then_inc(rmT_ps, 1)
                if k == HEAD + 2:
                    pe.wait_ge(diag_sb, b + 1)
                    mm(LB[0][:, 0:H], ones[:], diagR[:]).then_inc(Rb_ps, 1)
                if k == HEAD + 3:
                    pe.wait_ge(rho_n_sb, b + 1)
                if HEAD + 1 <= k < HEAD + 5:
                    for t in range(GT):
                        j = (k - HEAD - 1) * GT + t
                        ins = mm(LB[1][0:1, 0:D], tiny[:], hb[:, j, 0:D], start=(j == 0), stop=(j == JT - 1))
                    if j == JT - 1:
                        ins.then_inc(hsum_ps, 1)
                    if k == HEAD + 3:
                        T.transpose(LB[0][0:H * JT, 0:P], rho_n[:], ident[:]).then_inc(rho_ps, 1)

            def tile(b, g, ib, k, crossing):
                m = JT * g + k
                if k + LAG < JT:
                    transpose_adj(g, k + LAG)
                elif not is_last(g):
                    transpose_adj(g + 1, k + LAG - JT)
                if direct(k + 2, crossing):
                    if k + 2 == EARLY[0] and not (isinstance(g, int) and g == 0):
                        pe.wait_ge(nat_sb, 2 * g)
                    transpose_last_head(g, k + 2, BT_early if k + 2 in EARLY else BT_late)
                if k == 0:
                    if crossing:
                        pe.wait_ge(hmean_sb, b + 1)
                        pe.wait_ge(haug_sb, 2 * NC_ * b + 2)
                    if not (isinstance(g, int) and g == 0):
                        pe.wait_ge(accU_sb, 2 * g)
                    for h in range(H):
                        rows = slice(64 * (h % 2), 64 * (h % 2) + HA)
                        mm(ACC[h // 2][rows, :], hmean[:, h, :], ones_row[:], stop=False)
                if k == CHUNK and crossing:
                    pe.wait_ge(haug_sb, 2 * NC_ * (b + 1))
                pe.wait_ge(X_sb, m + 1)
                for h in range(H):
                    rows = slice(64 * (h % 2), 64 * (h % 2) + HA)
                    ins = mm(ACC[h // 2][rows, :], haug[:, k, h, :], X[k % NX][:, h, :], start=False, stop=(k == JT - 1))
                ins.then_inc(pv_done, 1)

            def epilogue(g, k):
                if k == 0:
                    pe.wait_ge(accU_sb, 2 * (g + 1))
                    for r in range(2):
                        for t in range(GT):
                            ins = T.transpose(LB[r][:, tsl(t)], accU[:, r, tsl(t)], ident[:])
                        ins.then_inc(nat_ps, 1)

            walk(pe, prepare, tile, epilogue)


_INS = ['x', 'adj', 'L0_gnn_W', 'L0_gnn_a', 'L0_gnn_ln_g', 'L0_gnn_ln_b', 'L0_gnn_W1', 'L0_gnn_b1', 'L0_gnn_W2',
        'L0_gnn_b2', 'L0_gnn_W3', 'L0_gnn_b3', 'L1_gnn_W_proj', 'L1_gnn_a_w', 'L1_gnn_bias']


def kernel(**inputs):
    import numpy as _np
    import concourse.bacc as _bacc
    from concourse import mybir as _mybir
    from concourse.bass_utils import run_bass_kernel_spmd as _run

    nc = _bacc.Bacc("TRN2", target_bir_lowering=False, num_devices=1)
    arrays, args = {}, []
    for name in _INS:
        a = _np.ascontiguousarray(inputs[name])
        arrays[f"in_{name}_dram"] = a
        args.append(nc.dram_tensor(f"in_{name}_dram", a.shape, _mybir.dt.from_np(a.dtype), kind="ExternalInput").ap())
    shape = tuple(inputs['x'].shape)
    args.append(nc.dram_tensor("out_0_dram", shape, _mybir.dt.float32, kind="ExternalOutput").ap())
    build_program(nc, *args)
    r = _run(nc, [arrays], core_ids=[0])
    return r.results[0]["out_0_dram"]
```
